# Optimizing a Trainium2 kernel written in Bass

```python
import numpy as np
import jax
import jax.numpy as jnp

def _softmax(x, axis=-1):
    return jax.nn.softmax(x, axis=axis)

def _gelu(x):
    return jax.nn.gelu(x, approximate=True)

def _silu(x):
    return jax.nn.silu(x)

def _sigmoid(x):
    return jax.nn.sigmoid(x)

def _layernorm(x, axis=-1, eps=1e-05):
    m = jnp.mean(x, axis=axis, keepdims=True)
    v = jnp.var(x, axis=axis, keepdims=True)
    return (x - m) / jnp.sqrt(v + eps)

def _scatter_add(tgt, idx, src, axis=0):
    return tgt.at[idx].add(src)

def _segment_sum(src, seg, n):
    return jax.ops.segment_sum(src, seg, n)
kernel_name = 'mk_adj_preln_d2_adj_r2_fa68f9'

def setup_inputs(seed: int=0):
    np.random.seed(seed)
    _w = jnp.asarray

    def _rec_inputs():
        import jax
        import jax.numpy as jnp
        _gk = jax.random.key(seed)
        x = 7.34e-05 + 1 * jax.random.normal(jax.random.fold_in(_gk, 1), (16, 512, 256), jnp.float32)
        _a = jax.random.bernoulli(jax.random.fold_in(_gk, 2), 0.03125, (512, 512))
        _a = jnp.logical_or(_a, jnp.swapaxes(_a, -1, -2))
        _a = jnp.logical_or(_a, jnp.eye(512, dtype=bool))
        _af = _a.astype(jnp.float32)
        adj = _af
        return (x, adj)
    x, adj = _rec_inputs()

    def _L0_gnn_setup():
        import jax, jax.numpy as jnp
        import numpy as np
        B, N, D, H = (16, 1025, 256, 8)
        LN_EPS = 1e-05

        def _make_mask(key, n):
            n_proto = n - 1
            adj = jax.random.bernoulli(key, 0.03, (n_proto, n_proto)).astype(jnp.float32)
            adj = jnp.clip(adj + adj.T + jnp.eye(n_proto, dtype=jnp.float32), 0.0, 1.0)
            mask = jnp.zeros((n, n), dtype=jnp.float32)
            mask = mask.at[0, :].set(1.0).at[:, 0].set(1.0)
            mask = mask.at[1:, 1:].set(adj)
            return mask
        key = jax.random.key(seed)
        ks = jax.random.split(key, 7)
        s = 1.0 / np.sqrt(D)
        return {'x': jax.random.normal(ks[0], (B, N, D), dtype=jnp.float32), 'w_qkv': jax.random.uniform(ks[1], (D, 3 * D), dtype=jnp.float32, minval=-s, maxval=s), 'w_proj': jax.random.uniform(ks[2], (D, D), dtype=jnp.float32, minval=-s, maxval=s), 'b_proj': jnp.zeros((D,), dtype=jnp.float32), 'ln_gamma': jnp.ones((D,), dtype=jnp.float32), 'ln_beta': jnp.zeros((D,), dtype=jnp.float32), 'attn_mask': _make_mask(ks[3], N)}
    _L0_gnn_all = _L0_gnn_setup()
    _L0_gnn_in = {k: v for k, v in _L0_gnn_all.items() if k in ('w_qkv', 'w_proj', 'b_proj', 'ln_gamma', 'ln_beta')}
    del _L0_gnn_all

    def _L1_gnn_setup():
        import jax, jax.numpy as jnp
        import numpy as np
        B, N, D, H = (4, 1024, 256, 8)
        HD = D // H
        key = jax.random.key(seed)
        ks = jax.random.split(key, 10)
        x = jax.random.normal(ks[0], (B, N, D), dtype=jnp.float32)
        adj = (jax.random.uniform(ks[1], (N, N)) < 0.1).astype(jnp.float32)
        s = 1.0 / np.sqrt(D)
        Wq = jax.random.normal(ks[2], (D, D), dtype=jnp.float32) * s
        Wk = jax.random.normal(ks[3], (D, D), dtype=jnp.float32) * s
        Wv = jax.random.normal(ks[4], (D, D), dtype=jnp.float32) * s
        Wo = jax.random.normal(ks[5], (D, D), dtype=jnp.float32) * s
        bq = jnp.zeros((D,), jnp.float32)
        bk = jnp.zeros((D,), jnp.float32)
        bv = jnp.zeros((D,), jnp.float32)
        bo = jnp.zeros((D,), jnp.float32)
        return {'x': x, 'adj': adj, 'Wq': Wq, 'bq': bq, 'Wk': Wk, 'bk': bk, 'Wv': Wv, 'bv': bv, 'Wo': Wo, 'bo': bo}
    _L1_gnn_all = _L1_gnn_setup()
    _L1_gnn_in = {k: v for k, v in _L1_gnn_all.items() if k in ('Wq', 'bq', 'Wk', 'bk', 'Wv', 'bv', 'Wo', 'bo')}
    del _L1_gnn_all
    return {'x': x, 'adj': adj, 'L0_gnn_w_qkv': _L0_gnn_in['w_qkv'], 'L0_gnn_w_proj': _L0_gnn_in['w_proj'], 'L0_gnn_b_proj': _L0_gnn_in['b_proj'], 'L0_gnn_ln_gamma': _L0_gnn_in['ln_gamma'], 'L0_gnn_ln_beta': _L0_gnn_in['ln_beta'], 'L1_gnn_Wq': _L1_gnn_in['Wq'], 'L1_gnn_bq': _L1_gnn_in['bq'], 'L1_gnn_Wk': _L1_gnn_in['Wk'], 'L1_gnn_bk': _L1_gnn_in['bk'], 'L1_gnn_Wv': _L1_gnn_in['Wv'], 'L1_gnn_bv': _L1_gnn_in['bv'], 'L1_gnn_Wo': _L1_gnn_in['Wo'], 'L1_gnn_bo': _L1_gnn_in['bo']}

def reference(x, adj, L0_gnn_w_qkv, L0_gnn_w_proj, L0_gnn_b_proj, L0_gnn_ln_gamma, L0_gnn_ln_beta, L1_gnn_Wq, L1_gnn_bq, L1_gnn_Wk, L1_gnn_bk, L1_gnn_Wv, L1_gnn_bv, L1_gnn_Wo, L1_gnn_bo):
    import jax
    import jax.numpy as jnp

    def _L0_gnn_ref(x, w_qkv, w_proj, b_proj, ln_gamma, ln_beta, attn_mask):
        import jax, jax.numpy as jnp
        import numpy as np
        B, N, D, H = (16, 1025, 256, 8)
        LN_EPS = 1e-05

        def _make_mask(key, n):
            n_proto = n - 1
            adj = jax.random.bernoulli(key, 0.03, (n_proto, n_proto)).astype(jnp.float32)
            adj = jnp.clip(adj + adj.T + jnp.eye(n_proto, dtype=jnp.float32), 0.0, 1.0)
            mask = jnp.zeros((n, n), dtype=jnp.float32)
            mask = mask.at[0, :].set(1.0).at[:, 0].set(1.0)
            mask = mask.at[1:, 1:].set(adj)
            return mask
        b, n, d = x.shape
        hd = d // H
        scale = hd ** (-0.5)
        qkv = (x @ w_qkv).reshape(b, n, 3, H, hd).transpose(2, 0, 3, 1, 4)
        q, k, v = (qkv[0], qkv[1], qkv[2])
        attn = jnp.einsum('bhnd,bhmd->bhnm', q, k) * scale
        attn = jnp.where(attn_mask[None, None] == 0, -jnp.inf, attn)
        attn = jax.nn.softmax(attn, axis=-1)
        o = jnp.einsum('bhnm,bhmd->bhnd', attn, v).transpose(0, 2, 1, 3).reshape(b, n, d)
        o = o @ w_proj + b_proj
        mu = jnp.mean(o, axis=-1, keepdims=True)
        var = jnp.mean(jnp.square(o - mu), axis=-1, keepdims=True)
        ln = (o - mu) * jax.lax.rsqrt(var + LN_EPS) * ln_gamma + ln_beta
        return o + ln

    def _L1_gnn_ref(x, adj, Wq, bq, Wk, bk, Wv, bv, Wo, bo):
        import jax, jax.numpy as jnp
        import numpy as np
        B, N, D, H = (4, 1024, 256, 8)
        HD = D // H
        b, n, d = x.shape
        q = (x @ Wq + bq).reshape(b, n, H, HD)
        k = (x @ Wk + bk).reshape(b, n, H, HD)
        v = (x @ Wv + bv).reshape(b, n, H, HD)
        scores = jnp.einsum('bqhd,bkhd->bhqk', q, k) / jnp.sqrt(jnp.float32(HD))
        scores = scores + (1.0 - adj)[None, None, :, :] * -1000000000.0
        attn = jax.nn.softmax(scores, axis=-1)
        out = jnp.einsum('bhqk,bkhd->bqhd', attn, v).reshape(b, n, d)
        return out @ Wo + bo
    h = jnp.maximum(_layernorm(x, axis=-1), 0.0)
    x = x + _L0_gnn_ref(h, L0_gnn_w_qkv, L0_gnn_w_proj, L0_gnn_b_proj, L0_gnn_ln_gamma, L0_gnn_ln_beta, adj)
    h = jnp.maximum(_layernorm(x, axis=-1), 0.0)
    x = x + _L1_gnn_ref(h, adj, L1_gnn_Wq, L1_gnn_bq, L1_gnn_Wk, L1_gnn_bk, L1_gnn_Wv, L1_gnn_bv, L1_gnn_Wo, L1_gnn_bo)
    return x

_drawn_inputs = setup_inputs


def setup_inputs(seed=0):
    import zlib

    import numpy as np

    out = dict(_drawn_inputs(seed))
    spreads = {'L0_gnn_b_proj': (0.0, 0.1),
     'L0_gnn_ln_gamma': (1.0, 0.2),
     'L0_gnn_ln_beta': (0.0, 0.1),
     'L1_gnn_bq': (0.0, 0.8),
     'L1_gnn_bk': (0.0, 0.8),
     'L1_gnn_bv': (0.0, 0.1),
     'L1_gnn_bo': (0.0, 0.1)}
    factors = {'L1_gnn_Wq': 4.149, 'L1_gnn_Wk': 3.932}
    for name, (base, spread) in spreads.items():
        noise = np.random.default_rng([zlib.crc32(name.encode()), seed]).standard_normal(out[name].shape)
        drawn = base * np.exp(spread * noise) if base else spread * noise
        out[name] = jnp.asarray(drawn.astype(out[name].dtype))
    for name, factor in factors.items():
        out[name] = (out[name] * factor).astype(out[name].dtype)
    return out
```

```python
import concourse.bass as bass
from concourse import mybir
from contextlib import ExitStack

F32, F16, BF16 = mybir.dt.float32, mybir.dt.float16, mybir.dt.bfloat16
ALU, ACT = mybir.AluOpType, mybir.ActivationFunctionType

PARTS = 128
BATCH, TOKENS, DIM, HEADS = 16, 512, 256, 8
HEAD = DIM // HEADS
UNITS = 2 * BATCH
TILES = TOKENS // PARTS
HALVES = DIM // PARTS
SLOTS, QUARTERS = HEADS, TILES
PAIRS = HEADS // 2
QK_TILES = 4
STACK = 3 * HEAD
W_SCALE = 256.0
ROOT = float(HEAD) ** 0.5
MASKED = -1.0e9 * ROOT
EPS = 1e-5
CONSTS = 16 * 9
QK_BANK = (1, 0, 0, 0)
LAID = 2
STACK_DMAS = 6 * 16


def twice(row):
    return row[:, :].unsqueeze(1).to_broadcast([PARTS, 2, DIM])


class Step:

    def __init__(self, c, i=None, layers=None):
        self.c, self.i, self.layers = c, i, layers

    def has(self, d):
        return self.i is not None or 0 <= self.c + d < UNITS

    def layer(self, d):
        return self.layers if self.i is not None else (self.c + d) // BATCH

    def parity(self, d):
        return (self.c + d) % 2

    def count(self, per_unit, d, extra=0):
        least = per_unit * (self.c + d) + extra
        return least if self.i is None else self.i * (2 * per_unit) + least

    def next(self):
        return Step(self.c + 1, self.i, self.layers)

    def unit(self, d):
        return self.c + d if self.i is None else self.i * 2 + (self.c + d)


def need(engine, semaphore, value):
    if not isinstance(value, int) or value > 0:
        engine.wait_ge(semaphore, value)


def run_steps(engine, step, change=14):
    for t in range(-3, 2):
        step(Step(t))
    with engine.Fori(1, change // 2) as i:
        step(Step(0, i, 0))
        step(Step(1, i, 0))
    for t in range(change, 17):
        step(Step(t))
    with engine.Fori(8, 14) as i:
        step(Step(1, i, 1))
        step(Step(2, i, 1))
    for t in range(29, UNITS + 1):
        step(Step(t))


def build(nc, x, adj, w_qkv0, w_out0, b_out0, gamma, beta, w_qkv1, b_q1, b_k1, b_v1, w_out1, b_out1, out):
    x1 = nc.dram_tensor("x1", [BATCH, TOKENS, DIM], F32).ap()
    w_qkv, w_out = (w_qkv0, w_qkv1), (w_out0, w_out1)

    def tokens(a, b):
        return a.rearrange("b (t p) d -> p b t d", p=PARTS)[:, bass.ds(b, 1), :, :].rearrange("p b t d -> p (b t) d")

    with ExitStack() as ctx:
        def sb(name, shape, dt):
            return ctx.enter_context(nc.sbuf_tensor(name, shape, dt))

        def ps(name):
            return ctx.enter_context(nc.psum_tensor(name, [PARTS, 512], F32))

        def sem(name):
            return ctx.enter_context(nc.semaphore(name))

        ident_f = sb("ident_f", [PARTS, PARTS], F32)
        ident_b = sb("ident_b", [PARTS, PARTS], BF16)
        ident_h = sb("ident_h", [PARTS, PARTS], F16)
        ones = sb("ones", [PARTS, HEAD], F32)
        eps = sb("eps", [PARTS, TILES], F32)
        minus_half = sb("minus_half", [PARTS, TILES], F32)
        mask_q = sb("mask_q", [PARTS, TILES, TOKENS], BF16)
        mask_k = sb("mask_k", [PARTS, TILES, TOKENS], BF16)
        w_hi = [sb(f"w_hi{n}", [PARTS, HALVES, 3 * DIM], F16) for n in range(2)]
        w_lo = [sb(f"w_lo{n}", [PARTS, HALVES, 3 * DIM], F16) for n in range(2)]
        w_o = [sb(f"w_o{n}", [PARTS, HALVES, DIM], F32) for n in range(2)]
        bias_o = [sb(f"bias_o{n}", [PARTS, DIM], F32) for n in range(2)]
        bias_v = sb("bias_v", [PARTS, DIM], F32)
        bias_qk = sb("bias_qk", [PARTS, QK_TILES], F32)
        gamma_b = sb("gamma_b", [PARTS, DIM], F32)
        beta_b = sb("beta_b", [PARTS, DIM], F32)
        flag = sb("flag", [1, 1], F32)
        x_in = sb("x_in", [PARTS, TILES, DIM], F32)
        stats = sb("stats", [PARTS, TILES, 6], F32)
        moments = sb("moments", [PARTS, TILES, 2], F32)
        var_eps = sb("var_eps", [PARTS, TILES], F32)
        rstd = sb("rstd", [PARTS, TILES], F32)
        shift = sb("shift", [PARTS, TILES], F32)
        h_full = sb("h_full", [PARTS, TILES, DIM], F32)
        h_hi = sb("h_hi", [PARTS, TILES, DIM], F16)
        h_lo = sb("h_lo", [PARTS, TILES, DIM], F16)
        ht_hi = [sb(f"ht_hi{n}", [PARTS, HALVES, TOKENS], F16) for n in range(2)]
        ht_lo = [sb(f"ht_lo{n}", [PARTS, HALVES, TOKENS], F16) for n in range(2)]
        qk_full = sb("qk_full", [PARTS, 2, TOKENS], F32)
        qk_hi = sb("qk_hi", [PARTS, QK_TILES, TOKENS], F16)
        qk_lo = sb("qk_lo", [PARTS, QK_TILES, TOKENS], F16)
        q_stack = [sb(f"q_stack{n}", [PARTS, HEADS, TOKENS], F16) for n in range(2)]
        k_stack = [sb(f"k_stack{n}", [PARTS, HEADS, TOKENS], F16) for n in range(2)]
        unused = sb("unused", [PARTS, 2, TOKENS], BF16)
        row_max = sb("row_max", [PARTS, HEADS, TILES], F32)
        neg_max = sb("neg_max", [4 * TILES, PARTS], F16)
        v = [sb(f"v{n}", [PARTS, TILES, DIM], F32) for n in range(2)]
        prob = sb("prob", [PARTS, HEADS, TILES, TOKENS], F32)
        half_sum = sb("half_sum", [PARTS, 2, TOKENS], F32)
        prob_sum = sb("prob_sum", [PARTS, HEADS, TOKENS], F32)
        heads_raw = sb("heads_raw", [PARTS, TOKENS], F32)
        recip = sb("recip", [PARTS, TOKENS], F32)
        heads_t = sb("heads_t", [PARTS, 2, TOKENS], F32)
        x_res = sb("x_res", [PARTS, TILES, DIM], F32)
        proj = sb("proj", [PARTS, TILES, DIM], F32)
        o_stats = sb("o_stats", [PARTS, TILES, 6], F32)
        o_moments = sb("o_moments", [PARTS, TILES, 2], F32)
        o_var = sb("o_var", [PARTS, TILES], F32)
        o_rstd = sb("o_rstd", [PARTS, TILES], F32)

        staging = prob[:, :, :, :].rearrange("p h k n -> p (h k n)")
        adj_in = staging[:, 0:TILES * TOKENS].rearrange("p (t n) -> p t n", t=TILES)
        W = HALVES * 3 * DIM
        w_in = [staging[:, 2048 + n * W:2048 + (n + 1) * W].rearrange("p (h n) -> p h n", h=HALVES)
                for n in range(2)]

        score_k = [ps(f"score_k{n}") for n in range(2)]
        score_q = [ps(f"score_q{n}") for n in range(2)]
        pv = ps("pv")
        denom = ps("denom")
        work = [ps(f"work{n}") for n in range(2)]

        adj_loaded, w_loaded, consts_loaded = sem("adj_loaded"), sem("w_loaded"), sem("consts_loaded")
        x_loaded = sem("x_loaded")
        res_loaded = sem("res_loaded")
        stored = sem("stored")
        pair_stacked = [sem(f"pair_stacked{j}") for j in range(PAIRS)]
        max_placed = [sem(f"max_placed{g}") for g in range(2)]
        zeroed, pool_consts, mask_made, mask_turned = (
            sem("zeroed"), sem("pool_consts"), sem("mask_made"), sem("mask_turned"))
        w_high, setup_done = sem("w_high"), sem("setup_done")
        stats_done, moments_done, var_done, rstd_done, shift_done = (
            sem("stats_done"), sem("moments_done"), sem("var_done"), sem("rstd_done"), sem("shift_done"))
        h_done, h_hi_done, h_lo_done = sem("h_done"), sem("h_hi_done"), sem("h_lo_done")
        turned, ht_hi_done, ht_lo_done = sem("turned"), sem("ht_hi_done"), sem("ht_lo_done")
        qk_ready, qk_full_done, qk_hi_done, qk_lo_done = (
            sem("qk_ready"), sem("qk_full_done"), sem("qk_hi_done"), sem("qk_lo_done"))
        score_q_ready, max_done = sem("score_q_ready"), sem("max_done")
        max_turned, neg_max_done = sem("max_turned"), sem("neg_max_done")
        v_ready, v_done = sem("v_ready"), sem("v_done")
        banks_marked, mask_laid = sem("banks_marked"), sem("mask_laid")
        score_k_ready, prob_done = sem("score_k_ready"), sem("prob_done")
        half_done, sum_done = sem("half_done"), sem("sum_done")
        pv_done, denom_ready = sem("pv_done"), sem("denom_ready")
        raw_done, recip_done, heads_done = sem("raw_done"), sem("recip_done"), sem("heads_done")
        proj_ready, proj_done = sem("proj_ready"), sem("proj_done")
        res_biased, res_added = sem("res_biased"), sem("res_added")
        o_stats_done, o_moments_done, o_var_done, o_rstd_done = (
            sem("o_stats_done"), sem("o_moments_done"), sem("o_var_done"), sem("o_rstd_done"))
        scaled_done, result_done = sem("scaled_done"), sem("result_done")

        block = ctx.enter_context(nc.Block())

        @block.sync
        def _(sp):
            sp.dma_start(adj_in, adj.rearrange("(t p) n -> p t n", p=PARTS)).then_inc(adj_loaded, 16)
            for n in range(2):
                sp.dma_start(w_in[n], w_qkv[n].rearrange("(h p) n -> p h n", p=PARTS)).then_inc(w_loaded, 16)
            for n, b_out in enumerate((b_out0, b_out1)):
                sp.dma_start(w_o[n][:], w_out[n].rearrange("(h p) n -> p h n", p=PARTS)).then_inc(consts_loaded, 16)
                sp.dma_start(bias_o[n][:], b_out.partition_broadcast(PARTS)).then_inc(consts_loaded, 16)
            sp.dma_start(bias_v[:], b_v1.partition_broadcast(PARTS)).then_inc(consts_loaded, 16)
            sp.dma_start(gamma_b[:], gamma.partition_broadcast(PARTS)).then_inc(consts_loaded, 16)
            sp.dma_start(beta_b[:], beta.partition_broadcast(PARTS)).then_inc(consts_loaded, 16)
            for n, b in enumerate((b_q1, b_k1)):
                sp.dma_start(bias_qk[:, 2 * n:2 * n + 2], b).then_inc(consts_loaded, 16)

            def stack_pair(t, d, j):
                rows = slice(HEAD * j, HEAD * (j + 1))
                for n, part in enumerate((qk_hi, qk_lo, qk_hi)):
                    sp.dma_start(q_stack[t.parity(d)][HEAD * n:HEAD * (n + 1), 2 * j:2 * j + 2, :],
                                 part[rows, 0:2, :]).then_inc(pair_stacked[j], 16)
                for n, part in enumerate((qk_hi, qk_hi, qk_lo)):
                    sp.dma_start(k_stack[t.parity(d)][HEAD * n:HEAD * (n + 1), 2 * j:2 * j + 2, :],
                                 part[rows, 2:4, :]).then_inc(pair_stacked[j], 16)

            def place_max(t, d, g):
                dst = q_stack[t.parity(d)][STACK:STACK + 1, 4 * g:4 * g + 4, :]
                sp.dma_start(dst.rearrange("o h (t n) -> o (h t) n", n=PARTS),
                             neg_max[:, :]).then_inc(max_placed[g], 16)

            def step(t):
                if t.has(3):
                    need(sp, h_done, t.count(1, 3))
                    src = x1 if t.layer(3) else x
                    b = t.unit(3) - BATCH * t.layer(3)
                    sp.dma_start(x_in[:], tokens(src, b)).then_inc(x_loaded, 16)
                if t.has(1):
                    need(sp, score_k_ready, t.count(32, 0))
                    stack_pair(t, 1, PAIRS - 1)
                if t.has(0):
                    need(sp, neg_max_done, t.count(2, 1))
                    place_max(t, 0, 1)
                if t.has(-1):
                    need(sp, stored, t.count(16, -1))
                    b = t.unit(-1) - BATCH * t.layer(-1)
                    src = x1 if t.layer(-1) else x
                    sp.dma_start(x_res[:], tokens(src, b)).then_inc(res_loaded, 16)
                if t.has(1):
                    need(sp, neg_max_done, t.count(2, 1, 1))
                    place_max(t, 1, 0)
                if t.has(2):
                    need(sp, qk_lo_done, t.count(4, 3))
                    for j in range(PAIRS - 1):
                        if j == 2 and t.has(0):
                            need(sp, score_k_ready, t.count(32, 0, 24))
                        stack_pair(t, 2, j)
                if t.has(-1):
                    need(sp, result_done, t.count(1, 0))
                    b = t.unit(-1) - BATCH * t.layer(-1)
                    dst = out if t.layer(-1) else x1
                    sp.dma_start(tokens(dst, b), x_res[:]).then_inc(stored, 16)

            run_steps(sp, step, BATCH - 4)
            sp.wait_ge(stored, 16 * UNITS)

        @block.gpsimd
        def _(pool):
            for n, m in enumerate((ident_f, ident_b, ident_h)):
                pool.memset(m[:], 0.0).then_inc(zeroed, 1)
            pool.memset(ones[:], 1.0).then_inc(pool_consts, 1)
            pool.memset(minus_half[:], -0.5).then_inc(pool_consts, 1)
            pool.memset(eps[:], EPS).then_inc(pool_consts, 1)
            pool.wait_ge(zeroed, 3)
            for m in (ident_f, ident_b, ident_h):
                pool.affine_select(out=m[:], in_=m[:], compare_op=ALU.not_equal, fill=1.0, base=0,
                                   pattern=[[-1, PARTS]], channel_multiplier=1).then_inc(pool_consts, 1)
            pool.wait_ge(pool_consts, 6)
            pool.wait_ge(consts_loaded, CONSTS)

            def reciprocal_root(t, var_in, var_out, root, semaphores, value):
                pool.tensor_tensor(var_out[:], var_in, eps[:], ALU.add).then_inc(semaphores[0], 1)
                pool.wait_ge(semaphores[0], value)
                pool.tensor_tensor(root[:], var_out[:], minus_half[:], ALU.pow).then_inc(semaphores[1], 1)

            def sum_head(t, h):
                need(pool, prob_done, t.count(32, 0, 4 * h + 4))
                need(pool, sum_done, t.count(8, 0, h))
                pool.tensor_tensor(half_sum[:], prob[:, h, 0:2, :], prob[:, h, 2:4, :], ALU.add).then_inc(half_done, 1)
                pool.wait_ge(half_done, t.count(8, 0, h + 1))
                need(pool, denom_ready, t.count(2, -1, h // 4 + 1))
                pool.tensor_tensor(prob_sum[:, h, :], half_sum[:, 0, :], half_sum[:, 1, :], ALU.add).then_inc(sum_done, 1)

            def step(t):
                for s in range(SLOTS):
                    if s == 1 and t.has(-1):
                        need(pool, res_loaded, t.count(16, 0))
                        for k in range(2):
                            add = twice(bias_o[1] if t.layer(-1) else beta_b)
                            pool.tensor_tensor(x_res[:, 2 * k:2 * k + 2, :], x_res[:, 2 * k:2 * k + 2, :], add,
                                               ALU.add).then_inc(res_biased, 1)
                    if s == 6 and t.has(3):
                        need(pool, moments_done, t.count(4, 4))
                        need(pool, h_done, t.count(1, 3))
                        reciprocal_root(t, moments[:, :, 1], var_eps, rstd, (var_done, rstd_done), t.count(1, 4))
                    if s == 7 and t.has(-1) and t.layer(-1) == 0:
                        need(pool, o_moments_done, t.count(4, 0))
                        need(pool, result_done, t.count(1, -1))
                        reciprocal_root(t, o_moments[:, :, 1], o_var, o_rstd, (o_var_done, o_rstd_done), t.count(1, 0))
                        need(pool, proj_done, t.count(2, 0))
                        need(pool, res_biased, t.count(2, 0))
                        pool.tensor_tensor(x_res[:], x_res[:], proj[:], ALU.add).then_inc(res_added, 1)
                    if t.has(0):
                        sum_head(t, s)

            run_steps(pool, step)

        @block.scalar
        def _(act):
            def h_of(t):
                need(act, shift_done, t.count(1, 3))
                need(act, h_lo_done, t.count(1, 2))
                for n in range(TILES):
                    last = nc.scalar.activation(h_full[:, n, :], x_in[:, n, :], ACT.Relu,
                                                bias=shift[:, n:n + 1], scale=rstd[:, n:n + 1])
                last.then_inc(h_done, 1)
                act.wait_ge(h_done, t.count(1, 3))
                need(act, turned, t.count(2, 2))
                nc.scalar.activation(h_hi[:], h_full[:], ACT.Copy).then_inc(h_hi_done, 1)

            def qk_of(t, m):
                need(act, qk_ready, t.count(4, 2, m + 1))
                need(act, qk_lo_done, t.count(4, 2, m - 1))
                bias = bias_qk[:, m:m + 1] if t.layer(2) else 0.0
                nc.scalar.activation(qk_full[:, m % 2, :], work[QK_BANK[m]][:], ACT.Identity, bias=bias,
                                     scale=1.0 / W_SCALE).then_inc(qk_full_done, 1)
                for j in range(PAIRS):
                    need(act, pair_stacked[j], t.count(STACK_DMAS, 2))
                nc.scalar.activation(qk_hi[:, m, :], work[QK_BANK[m]][:], ACT.Identity, bias=bias,
                                     scale=1.0 / W_SCALE).then_inc(qk_hi_done, 1)

            def lay_mask(t, n):
                s, q = divmod(n, QUARTERS)
                if q < LAID:
                    need(act, prob_done, t.count(32, 0, n - 1))
                    nc.scalar.activation(score_k[q % 2][:], mask_k[:, q, :], ACT.Copy).then_inc(mask_laid, 1)

            def step(t):
                for s in range(SLOTS):
                    for q in range(QUARTERS):
                        if s == 0 and q == 0 and t.has(2):
                            h_of(t)
                        if s == 2 and q == 0 and t.has(2):
                            need(act, turned, t.count(2, 3))
                            need(act, v_ready, t.count(2, 1) if t.has(0) else 0)
                            nc.scalar.activation(ht_lo[t.parity(2)][:].rearrange("p h n -> p (h n)"),
                                                 work[0][:].bitcast(F16), ACT.Copy).then_inc(ht_lo_done, 1)
                        if 3 <= s < 3 + QK_TILES and q == 0 and t.has(2):
                            qk_of(t, s - 3)
                        if t.has(0):
                            need(act, score_k_ready, t.count(32, 0, 4 * s + q + 1))
                            if q == 0:
                                need(act, pv_done, t.count(8, -1, 4 * (s // 4 + 1)))
                                need(act, half_done, t.count(8, -1, s + 1))
                            nc.scalar.activation(prob[:, s, q, :], score_k[q % 2][:], ACT.Exp,
                                                 scale=1.0 / ROOT).then_inc(prob_done, 1)
                        n = 4 * s + q + 2
                        if n < 32 and t.has(0):
                            lay_mask(t, n)
                        if n >= 32 and t.has(1):
                            lay_mask(t.next(), n - 32)
                        if q == 3 and ((s == 3 and t.has(-1)) or (s == 7 and t.has(0))):
                            done = t.count(2, 0) if s == 3 else t.count(2, 0, 1)
                            need(act, pv_done, t.count(8, 0) if s == 3 else t.count(8, 0, 4))
                            need(act, heads_done, done - 1)
                            nc.scalar.activation(heads_raw[:], pv[:], ACT.Copy).then_inc(raw_done, 1)

            act.wait_ge(setup_done, 6)
            act.wait_ge(banks_marked, 1)
            run_steps(act, step)

        @block.vector
        def _(dve):
            tiles_asked = dve.alloc_register("tiles_asked")
            dve.reg_mov(tiles_asked, 0)
            for n in range(2):
                nc.vector.memset(k_stack[n][STACK:STACK + 1, :, :], 1.0).then_inc(setup_done, 1)
            dve.wait_ge(adj_loaded, 16)
            nc.vector.tensor_scalar(mask_q[:], adj_in, 0.0, MASKED, ALU.is_equal, ALU.mult).then_inc(mask_made, 1)
            dve.wait_ge(w_loaded, 32)
            for n in range(2):
                nc.vector.tensor_scalar(w_hi[n][:], w_in[n], W_SCALE, None, ALU.mult).then_inc(w_high, 1)
                dve.wait_ge(w_high, n + 1)
                nc.vector.scalar_tensor_tensor(
                    w_lo[n][:].rearrange("p h n -> p (h n)"), w_in[n].rearrange("p h n -> p (h n)"), W_SCALE,
                    w_hi[n][:].rearrange("p h n -> p (h n)"), ALU.mult, ALU.subtract).then_inc(setup_done, 1)
            for n in range(2):
                dve.wait_ge(mask_turned, n + 1)
                nc.vector.tensor_copy(mask_k[:, 2 * n:2 * n + 2, :].rearrange("p t n -> p (t n)"),
                                      work[n][:].bitcast(BF16)).then_inc(setup_done, 1)
            dve.wait_ge(setup_done, 6)
            dve.wait_ge(consts_loaded, CONSTS)
            dve.wait_ge(pool_consts, 6)

            def statistics(t, source, st, mom, semaphores, counts, free):
                for n in range(TILES):
                    if n == 0:
                        for semaphore, value in free:
                            need(dve, semaphore, value)
                    nc.vector.bn_stats(st[:, n, :], source[:, n, :]).then_inc(semaphores[0], 1)
                dve.wait_ge(semaphores[0], counts + TILES)
                nc.vector.memset(flag[:], 0.0)
                for n in range(TILES):
                    nc.vector.bn_aggr(mom[:, n, :], st[:, n, :]).then_inc(semaphores[1], 1)

            def max_of(t, s, q):
                if q == 0 and s % 4 == 0:
                    need(dve, max_turned, t.count(2, 0, s // 4 + 1))
                dve.reg_add(tiles_asked, tiles_asked, 1)
                dve.wait_ge(setup_done, 6)
                dve.wait_ge(score_q_ready, tiles_asked)
                nc.vector.tensor_tensor_reduce(out=unused[:, q % 2, :], in0=score_q[q % 2][:], in1=mask_q[:, q, :],
                                               scale=1.0, scalar=-3.0e38, op0=ALU.add, op1=ALU.max,
                                               accum_out=row_max[:, s, q:q + 1]).then_inc(max_done, 1)

            def negate_max(t, d, g):
                need(dve, max_turned, t.count(2, d, g + 1))
                need(dve, max_placed[1 - g], t.count(16, d, 16 * g))
                nc.vector.tensor_scalar(neg_max[:], work[1 - g][0:4 * TILES, 0:PARTS], -1.0, None,
                                        ALU.mult).then_inc(neg_max_done, 1)

            def normalise(t, d, g):
                index = t.count(2, d, g)
                need(dve, denom_ready, index + 1)
                need(dve, heads_done, index)
                nc.vector.reciprocal(recip[:], denom[:]).then_inc(recip_done, 1)
                need(dve, recip_done, index + 1)
                need(dve, raw_done, index + 1)
                need(dve, proj_ready, t.count(2, d))
                nc.vector.tensor_tensor(heads_t[:, g, :], heads_raw[:], recip[:], ALU.mult).then_inc(heads_done, 1)

            def take_v(t, k):
                need(dve, v_ready, t.count(2, 1, k + 1))
                need(dve, pv_done, t.count(8, 0))
                dst = v[t.parity(1)][:, 2 * k:2 * k + 2, :]
                bank = work[1][:].rearrange("p (t n) -> p t n", t=2)
                if t.layer(1):
                    nc.vector.scalar_tensor_tensor(dst, bank, 1.0 / W_SCALE, twice(bias_v),
                                                   ALU.mult, ALU.add).then_inc(v_done, 1)
                else:
                    nc.vector.tensor_scalar(dst, bank, 1.0 / W_SCALE, None, ALU.mult).then_inc(v_done, 1)

            def take_projection(t, k):
                need(dve, proj_ready, t.count(2, -1, k + 1))
                tiles = slice(2 * k, 2 * k + 2)
                bank = work[1 - k][:].rearrange("p (t n) -> p t n", t=2)
                if t.layer(-1):
                    need(dve, res_biased, t.count(2, -1, k + 1))
                    nc.vector.tensor_tensor(x_res[:, tiles, :], bank, x_res[:, tiles, :], ALU.add
                                            ).then_inc(proj_done, 1)
                    if k == 1:
                        need(dve, proj_done, t.count(2, 0))
                        nc.vector.memset(flag[:], 0.0).then_inc(result_done, 1)
                else:
                    need(dve, result_done, t.count(1, -1))
                    nc.vector.tensor_tensor(proj[:, tiles, :], bank, twice(bias_o[0]), ALU.add).then_inc(proj_done, 1)

            def finish_layer_0(t):
                need(dve, res_added, t.count(1, 0))
                for n in range(TILES):
                    nc.vector.scalar_tensor_tensor(proj[:, n, :], proj[:, n, :], o_moments[:, n, 0:1], gamma_b[:],
                                                   ALU.subtract, ALU.mult).then_inc(scaled_done, 1)
                need(dve, o_rstd_done, t.count(1, 0))
                for n in range(TILES):
                    need(dve, scaled_done, t.count(4, -1, n + 1))
                    last = nc.vector.scalar_tensor_tensor(x_res[:, n, :], proj[:, n, :], o_rstd[:, n:n + 1],
                                                          x_res[:, n, :], ALU.mult, ALU.add)
                last.then_inc(result_done, 1)

            def step(t):
                for s in range(SLOTS):
                    for q in range(QUARTERS):
                        if t.has(1):
                            max_of(t, s, q)
                        if (s, q) == (0, 2) and t.has(0):
                            negate_max(t, 0, 1)
                        if (s, q) == (0, 3) and t.has(2):
                            need(dve, h_hi_done, t.count(1, 3))
                            need(dve, turned, t.count(2, 2))
                            nc.vector.tensor_tensor(h_lo[:], h_full[:], h_hi[:], ALU.subtract).then_inc(h_lo_done, 1)
                        if (s, q) == (2, 0) and t.has(2):
                            need(dve, turned, t.count(2, 2, 1))
                            need(dve, v_ready, t.count(2, 1) if t.has(0) else 0)
                            nc.vector.tensor_copy(ht_hi[t.parity(2)][:].rearrange("p h n -> p (h n)"),
                                                  work[1][:].bitcast(F16)).then_inc(ht_hi_done, 1)
                        if 3 <= s < 3 + QK_TILES and q == 2 and t.has(2):
                            m = s - 3
                            need(dve, qk_hi_done, t.count(4, 2, m + 1))
                            for j in range(PAIRS):
                                need(dve, pair_stacked[j], t.count(STACK_DMAS, 2))
                            nc.vector.tensor_tensor(qk_lo[:, m, :], qk_full[:, m % 2, :], qk_hi[:, m, :],
                                                    ALU.subtract).then_inc(qk_lo_done, 1)
                        if (s, q) == (4, 0) and t.has(-1):
                            normalise(t, -1, 1)
                        if (s, q) == (4, 2) and t.has(1):
                            negate_max(t, 1, 0)
                        if (s, q) == (5, 3) and t.has(-1):
                            take_projection(t, 0)
                        if (s, q) == (6, 2) and t.has(3):
                            need(dve, x_loaded, t.count(16, 4))
                            statistics(t, x_in, stats, moments, (stats_done, moments_done),
                                       t.count(4, 3), ((moments_done, t.count(4, 3)), (shift_done, t.count(1, 3))))
                        if (s, q) == (7, 0) and t.has(-1):
                            take_projection(t, 1)
                        if (s, q) == (7, 0) and t.has(1):
                            take_v(t, 0)
                        if (s, q) == (7, 1) and t.has(-1) and t.layer(-1) == 0:
                            need(dve, proj_done, t.count(2, 0))
                            statistics(t, proj, o_stats, o_moments, (o_stats_done, o_moments_done), t.count(4, -1),
                                       ((o_moments_done, t.count(4, -1)), (scaled_done, t.count(4, -1)),
                                        (o_rstd_done, t.count(1, -1))))
                        if (s, q) == (7, 2) and t.has(3):
                            need(dve, rstd_done, t.count(1, 4))
                            nc.vector.scalar_tensor_tensor(shift[:], moments[:, :, 0], -1.0, rstd[:],
                                                           ALU.mult, ALU.mult).then_inc(shift_done, 1)
                if t.has(1):
                    take_v(t, 1)
                if t.has(0):
                    normalise(t, 0, 0)
                if t.has(-1) and t.layer(-1) == 0:
                    finish_layer_0(t)

            run_steps(dve, step)

        @block.tensor
        def _(pe):
            pe.wait_ge(pool_consts, 6)
            pe.wait_ge(mask_made, 1)
            for n in range(2):
                turned_mask = work[n][:].bitcast(BF16).rearrange("p (t n) -> p t n", t=2)
                for k in range(2):
                    for q in range(TILES):
                        key = PARTS * (2 * n + k)
                        last = nc.tensor.transpose(turned_mask[:, k, PARTS * q:PARTS * (q + 1)],
                                                   mask_q[:, q, key:key + PARTS], ident_b[:])
                last.then_inc(mask_turned, 1)
            pe.wait_ge(setup_done, 6)
            pe.wait_ge(consts_loaded, CONSTS)
            for bank in score_k:
                last = nc.tensor.matmul(bank[:], ident_b[:], mask_k[:, 0, :], start=True, stop=True)
            last.then_inc(banks_marked, 1)

            def scores_by_key(t, s, q):
                if s % 4 == 0 and q == 0:
                    need(pe, max_placed[s // 4], t.count(16, 1))
                bank = score_k[q % 2]
                if q < LAID:
                    need(pe, mask_laid, t.count(LAID * SLOTS, 0, LAID * s + q + 1))
                else:
                    need(pe, prob_done, t.count(32, 0, 4 * s + q - 1))
                    nc.tensor.matmul(bank[:], ident_b[:], mask_k[:, q, :], start=True, stop=False)
                nc.tensor.matmul(bank[:], k_stack[t.parity(0)][0:STACK + 1, s, PARTS * q:PARTS * (q + 1)],
                                 q_stack[t.parity(0)][0:STACK + 1, s, :], start=False, stop=True,
                                 skip_group_check=q < LAID).then_inc(score_k_ready, 1)

            def scores_by_query(t, s, q):
                if s % 2 == 0 and q == 0:
                    need(pe, pair_stacked[s // 2], t.count(STACK_DMAS, 2))
                need(pe, max_done, t.count(32, 1, 4 * s + q - 1))
                nc.tensor.matmul(score_q[q % 2][:], q_stack[t.parity(1)][0:STACK, s, PARTS * q:PARTS * (q + 1)],
                                 k_stack[t.parity(1)][0:STACK, s, :], start=True, stop=True
                                 ).then_inc(score_q_ready, 1)

            def times_v(t, d, g, k):
                if k == 0:
                    need(pe, prob_done, t.count(32, d, 16 * (g + 1)))
                    need(pe, v_done, t.count(2, d + 1))
                    need(pe, raw_done, t.count(2, d, g))
                for j in range(4):
                    h = 4 * g + j
                    last = nc.tensor.matmul(pv[HEAD * j:HEAD * (j + 1), :], v[t.parity(d)][:, k, HEAD * h:HEAD * (h + 1)],
                                            prob[:, h, k, :], start=(k == 0), stop=(k == TILES - 1))
                last.then_inc(pv_done, 1)

            def sum_rows(t, d, g):
                need(pe, sum_done, t.count(8, d, 4 * (g + 1)))
                need(pe, recip_done, t.count(2, d, g))
                for j in range(4):
                    last = nc.tensor.matmul(denom[HEAD * j:HEAD * (j + 1), :], ones[:], prob_sum[:, 4 * g + j, :],
                                            start=True, stop=True)
                last.then_inc(denom_ready, 1)

            def turn_h(t, part, bank):
                dst = work[bank][:].bitcast(F16).rearrange("p (h n) -> p h n", h=HALVES)
                for k in range(HALVES):
                    for n in range(TILES):
                        last = nc.tensor.transpose(dst[:, k, PARTS * n:PARTS * (n + 1)],
                                                   part[:, n, PARTS * k:PARTS * (k + 1)], ident_h[:])
                last.then_inc(turned, 1)

            def qk_terms(t):
                hi, lo = w_hi[t.layer(2)], w_lo[t.layer(2)]
                p = t.parity(2)
                return [(w, ht, k) for w, ht in ((hi, ht_hi[p]), (lo, ht_hi[p]), (hi, ht_lo[p])) for k in range(HALVES)]

            def project_qk(t, m, part):
                terms = qk_terms(t)
                for n in range(3 * part, 3 * part + 3):
                    w, ht, k = terms[n]
                    last = nc.tensor.matmul(work[QK_BANK[m]][:], w[:, k, PARTS * m:PARTS * (m + 1)], ht[:, k, :],
                                            start=(n == 0), stop=(n == 5))
                if part == 1:
                    last.then_inc(qk_ready, 1)

            def project_v(t, n):
                hi, lo = w_hi[t.layer(1)], w_lo[t.layer(1)]
                p = t.parity(1)
                terms = [(w, ht, k) for w, ht in ((hi, ht_hi[p]), (lo, ht_hi[p]), (hi, ht_lo[p])) for k in range(HALVES)]
                dst = work[1][:].rearrange("p (t n) -> p t n", t=2)[:, n % 2, :]
                for i, (w, ht, k) in enumerate(terms):
                    last = nc.tensor.matmul(dst, ht[:, k, PARTS * n:PARTS * (n + 1)], w[:, k, 2 * DIM:3 * DIM],
                                            start=(i == 0), stop=(i == 5))
                if n % 2:
                    last.then_inc(v_ready, 1)

            def turn_max(t, d, g):
                need(pe, max_done, t.count(32, d, 16 * (g + 1)))
                nc.tensor.matmul(work[1 - g][0:4 * TILES, 0:PARTS],
                                 row_max[:, 4 * g:4 * g + 4, :].rearrange("p h t -> p (h t)"), ident_f[:],
                                 start=True, stop=True).then_inc(max_turned, 1)

            def project_out(t, k):
                dst = work[1 - k][:].rearrange("p (t n) -> p t n", t=2)
                for n in range(2):
                    for half in range(HALVES):
                        tile = PARTS * (2 * k + n)
                        last = nc.tensor.matmul(dst[:, n, :], heads_t[:, half, tile:tile + PARTS],
                                                w_o[t.layer(-1)][:, half, :], start=(half == 0), stop=(half == 1))
                last.then_inc(proj_ready, 1)

            def banks_free(t):
                for semaphore, per, d, extra in ((ht_hi_done, 1, 2, 0), (ht_lo_done, 1, 2, 0), (qk_hi_done, 4, 2, 0),
                                                 (v_done, 2, 1, 0), (neg_max_done, 2, 0, 1), (proj_done, 2, -1, 0)):
                    need(pe, semaphore, min(t.count(per, d, extra), per * UNITS))

            def step(t):
                if t.i is None and (t.c < 1 or t.c > UNITS - 4):
                    banks_free(t)
                for s in range(SLOTS):
                    for q in range(QUARTERS):
                        if t.has(0):
                            scores_by_key(t, s, q)
                        if t.has(1):
                            scores_by_query(t, s, q)
                        if q == 0 and s < 4 and t.has(-1):
                            times_v(t, -1, 1, s)
                        if q == 0 and s >= 4 and t.has(0):
                            times_v(t, 0, 0, s - 4)
                        if (s, q) == (3, 1) and t.has(-1):
                            sum_rows(t, -1, 1)
                        if (s, q) == (7, 1) and t.has(0):
                            sum_rows(t, 0, 0)
                        if (s, q) == (0, 1) and t.has(0):
                            need(pe, proj_done, t.count(2, -1))
                            turn_max(t, 0, 1)
                        if (s, q) == (1, 2) and t.has(2):
                            need(pe, h_hi_done, t.count(1, 3))
                            need(pe, v_done, t.count(2, 1))
                            turn_h(t, h_hi, 1)
                        if (s, q) == (1, 3) and t.has(2):
                            need(pe, h_lo_done, t.count(1, 3))
                            need(pe, neg_max_done, t.count(2, 1) if t.has(0) else 0)
                            turn_h(t, h_lo, 0)
                        if 2 <= s < 2 + QK_TILES and q == 2 and t.has(2):
                            m = s - 2
                            if m == 0:
                                need(pe, ht_hi_done, t.count(1, 3))
                                need(pe, ht_lo_done, t.count(1, 3))
                            if m >= 1:
                                need(pe, qk_hi_done, t.count(4, 2, m))
                            project_qk(t, m, 0)
                        if 2 <= s < 2 + QK_TILES and q == 3 and t.has(2):
                            project_qk(t, s - 2, 1)
                        if (s, q) == (4, 1) and t.has(1):
                            if t.has(2):
                                need(pe, qk_hi_done, t.count(4, 2, 1))
                            turn_max(t, 1, 0)
                        if (s, q) == (5, 1) and t.has(-1):
                            need(pe, heads_done, t.count(2, 0))
                            if t.has(1):
                                need(pe, neg_max_done, t.count(2, 1, 1))
                            project_out(t, 0)
                        if s == 6 and q in (1, 2) and t.has(1):
                            if q == 1:
                                if t.has(-1):
                                    need(pe, proj_done, t.count(2, -1, 1))
                                else:
                                    need(pe, neg_max_done, t.count(2, 1, 1))
                            project_v(t, q - 1)
                        if (s, q) == (6, 3) and t.has(-1):
                            if t.has(2):
                                need(pe, qk_hi_done, t.count(4, 3))
                            elif t.has(0):
                                need(pe, neg_max_done, t.count(2, 1))
                            project_out(t, 1)
                        if s == 7 and q in (2, 3) and t.has(1):
                            if q == 2:
                                need(pe, v_done, t.count(2, 1, 1))
                            project_v(t, q)

            run_steps(pe, step)


def kernel(**inputs):
    import numpy as np
    import concourse.bacc as bacc
    from concourse import mybir
    from concourse.bass_utils import run_bass_kernel_spmd

    def even_odd(w):
        return np.concatenate([w.reshape(DIM, PAIRS, 2, HEAD)[:, :, g, :].reshape(DIM, -1) for g in range(2)], 1)

    def by_head_tile(b):
        return np.ascontiguousarray(b.reshape(PAIRS, 2, HEAD).transpose(0, 2, 1).reshape(-1, 2))

    a = {name: np.asarray(value) for name, value in inputs.items()}
    w0 = a["L0_gnn_w_qkv"]
    arrays = {
        "x": a["x"], "adj": a["adj"],
        "w_qkv0": np.concatenate([even_odd(w0[:, :DIM]), even_odd(w0[:, DIM:2 * DIM]), w0[:, 2 * DIM:]], 1),
        "w_out0": a["L0_gnn_w_proj"], "b_out0": a["L0_gnn_b_proj"],
        "gamma": a["L0_gnn_ln_gamma"], "beta": a["L0_gnn_ln_beta"],
        "w_qkv1": np.concatenate([even_odd(a["L1_gnn_Wq"]), even_odd(a["L1_gnn_Wk"]), a["L1_gnn_Wv"]], 1),
        "b_q1": by_head_tile(a["L1_gnn_bq"]), "b_k1": by_head_tile(a["L1_gnn_bk"]), "b_v1": a["L1_gnn_bv"],
        "w_out1": a["L1_gnn_Wo"], "b_out1": a["L1_gnn_bo"],
    }
    nc = bacc.Bacc("TRN2", target_bir_lowering=False, num_devices=1)
    args = {}
    for name, value in arrays.items():
        arrays[name] = np.ascontiguousarray(value)
        args[name] = nc.dram_tensor(name, value.shape, mybir.dt.from_np(value.dtype), kind="ExternalInput").ap()
    out = nc.dram_tensor("out", (BATCH, TOKENS, DIM), mybir.dt.float32, kind="ExternalOutput").ap()
    build(nc, out=out, **args)
    r = run_bass_kernel_spmd(nc, [arrays], core_ids=[0])
    return r.results[0]["out"]
```

```python
import concourse.bass as bass
from concourse import mybir
from contextlib import ExitStack

F32, F16, BF16 = mybir.dt.float32, mybir.dt.float16, mybir.dt.bfloat16
ALU, ACT = mybir.AluOpType, mybir.ActivationFunctionType

PARTS = 128
BATCH, TOKENS, DIM, HEADS = 16, 512, 256, 8
HEAD = DIM // HEADS
UNITS = 2 * BATCH
TILES = TOKENS // PARTS
HALVES = DIM // PARTS
SLOTS, QUARTERS = HEADS, TILES
PAIRS = HEADS // 2
QK_TILES = 4
STACK = 3 * HEAD
W_SCALE = 256.0
ROOT = float(HEAD) ** 0.5
MASKED = -1.0e9 * ROOT
EPS = 1e-5
CONSTS = 16 * 9
QK_BANK = (1, 0, 0, 0)
LAID = 2
STACK_DMAS = 6 * 16


def twice(row):
    return row[:, :].unsqueeze(1).to_broadcast([PARTS, 2, DIM])


class Step:

    def __init__(self, c, i=None, layers=None):
        self.c, self.i, self.layers = c, i, layers

    def has(self, d):
        return self.i is not None or 0 <= self.c + d < UNITS

    def layer(self, d):
        return self.layers if self.i is not None else (self.c + d) // BATCH

    def parity(self, d):
        return (self.c + d) % 2

    def count(self, per_unit, d, extra=0):
        least = per_unit * (self.c + d) + extra
        return least if self.i is None else self.i * (2 * per_unit) + least

    def next(self):
        return Step(self.c + 1, self.i, self.layers)

    def unit(self, d):
        return self.c + d if self.i is None else self.i * 2 + (self.c + d)


def need(engine, semaphore, value):
    if not isinstance(value, int) or value > 0:
        engine.wait_ge(semaphore, value)


def run_steps(engine, step, change=14):
    for t in range(-3, 2):
        step(Step(t))
    with engine.Fori(1, change // 2) as i:
        step(Step(0, i, 0))
        step(Step(1, i, 0))
    for t in range(change, 18):
        step(Step(t))
    with engine.Fori(9, 14) as i:
        step(Step(0, i, 1))
        step(Step(1, i, 1))
    for t in range(28, UNITS + 1):
        step(Step(t))


def build(nc, x, adj, w_qkv0, w_out0, b_out0, gamma, beta, w_qkv1, b_q1, b_k1, b_v1, w_out1, b_out1, out):
    x1 = nc.dram_tensor("x1", [BATCH, TOKENS, DIM], F32).ap()
    w_qkv, w_out = (w_qkv0, w_qkv1), (w_out0, w_out1)

    def tokens(a, b):
        return a.rearrange("b (t p) d -> p b t d", p=PARTS)[:, bass.ds(b, 1), :, :].rearrange("p b t d -> p (b t) d")

    with ExitStack() as ctx:
        def sb(name, shape, dt):
            return ctx.enter_context(nc.sbuf_tensor(name, shape, dt))

        def ps(name):
            return ctx.enter_context(nc.psum_tensor(name, [PARTS, 512], F32))

        def sem(name):
            return ctx.enter_context(nc.semaphore(name))

        ident_f = sb("ident_f", [PARTS, PARTS], F32)
        ident_b = sb("ident_b", [PARTS, PARTS], BF16)
        ident_h = sb("ident_h", [PARTS, PARTS], F16)
        ones = sb("ones", [PARTS, HEAD], F32)
        eps = sb("eps", [PARTS, TILES], F32)
        minus_half = sb("minus_half", [PARTS, TILES], F32)
        mask_q = sb("mask_q", [PARTS, TILES, TOKENS], BF16)
        mask_k = sb("mask_k", [PARTS, TILES, TOKENS], BF16)
        w_hi = [sb(f"w_hi{n}", [PARTS, HALVES, 3 * DIM], F16) for n in range(2)]
        w_lo = [sb(f"w_lo{n}", [PARTS, HALVES, 3 * DIM], F16) for n in range(2)]
        w_o = [sb(f"w_o{n}", [PARTS, HALVES, DIM], F32) for n in range(2)]
        bias_o = [sb(f"bias_o{n}", [PARTS, DIM], F32) for n in range(2)]
        bias_v = sb("bias_v", [PARTS, DIM], F32)
        bias_qk = sb("bias_qk", [PARTS, QK_TILES], F32)
        gamma_b = sb("gamma_b", [PARTS, DIM], F32)
        beta_b = sb("beta_b", [PARTS, DIM], F32)
        flag = sb("flag", [1, 1], F32)
        x_in = sb("x_in", [PARTS, TILES, DIM], F32)
        stats = sb("stats", [PARTS, TILES, 6], F32)
        moments = sb("moments", [PARTS, TILES, 2], F32)
        var_eps = sb("var_eps", [PARTS, TILES], F32)
        rstd = sb("rstd", [PARTS, TILES], F32)
        shift = sb("shift", [PARTS, TILES], F32)
        h_full = sb("h_full", [PARTS, TILES, DIM], F32)
        h_hi = sb("h_hi", [PARTS, TILES, DIM], F16)
        h_lo = sb("h_lo", [PARTS, TILES, DIM], F16)
        ht_hi = [sb(f"ht_hi{n}", [PARTS, HALVES, TOKENS], F16) for n in range(2)]
        ht_lo = [sb(f"ht_lo{n}", [PARTS, HALVES, TOKENS], F16) for n in range(2)]
        qk_full = sb("qk_full", [PARTS, 2, TOKENS], F32)
        qk_hi = sb("qk_hi", [PARTS, QK_TILES, TOKENS], F16)
        qk_lo = sb("qk_lo", [PARTS, QK_TILES, TOKENS], F16)
        q_stack = [sb(f"q_stack{n}", [PARTS, HEADS, TOKENS], F16) for n in range(2)]
        k_stack = [sb(f"k_stack{n}", [PARTS, HEADS, TOKENS], F16) for n in range(2)]
        unused = sb("unused", [PARTS, 2, TOKENS], BF16)
        row_max = sb("row_max", [PARTS, HEADS, TILES], F32)
        neg_max = sb("neg_max", [4 * TILES, PARTS], F16)
        v = [sb(f"v{n}", [PARTS, TILES, DIM], F32) for n in range(2)]
        prob = sb("prob", [PARTS, HEADS, TILES, TOKENS], F32)
        half_sum = sb("half_sum", [PARTS, 2, TOKENS], F32)
        prob_sum = sb("prob_sum", [PARTS, HEADS, TOKENS], F32)
        heads_raw = sb("heads_raw", [PARTS, TOKENS], F32)
        recip = sb("recip", [PARTS, TOKENS], F32)
        heads_t = sb("heads_t", [PARTS, 2, TOKENS], F32)
        x_res = sb("x_res", [PARTS, TILES, DIM], F32)
        proj = sb("proj", [PARTS, TILES, DIM], F32)
        o_stats = sb("o_stats", [PARTS, TILES, 6], F32)
        o_moments = sb("o_moments", [PARTS, TILES, 2], F32)
        o_var = sb("o_var", [PARTS, TILES], F32)
        o_rstd = sb("o_rstd", [PARTS, TILES], F32)

        staging = prob[:, :, :, :].rearrange("p h k n -> p (h k n)")
        adj_in = staging[:, 0:TILES * TOKENS].rearrange("p (t n) -> p t n", t=TILES)
        W = HALVES * 3 * DIM
        w_in = [staging[:, 2048 + n * W:2048 + (n + 1) * W].rearrange("p (h n) -> p h n", h=HALVES)
                for n in range(2)]

        score_k = [ps(f"score_k{n}") for n in range(2)]
        score_q = [ps(f"score_q{n}") for n in range(2)]
        pv = ps("pv")
        denom = ps("denom")
        work = [ps(f"work{n}") for n in range(2)]

        adj_loaded, w_loaded, consts_loaded = sem("adj_loaded"), sem("w_loaded"), sem("consts_loaded")
        x_loaded = sem("x_loaded")
        res_loaded = sem("res_loaded")
        stored = sem("stored")
        pair_stacked = [sem(f"pair_stacked{j}") for j in range(PAIRS)]
        max_placed = [sem(f"max_placed{g}") for g in range(2)]
        zeroed, pool_consts, mask_made, mask_turned = (
            sem("zeroed"), sem("pool_consts"), sem("mask_made"), sem("mask_turned"))
        w_high, setup_done = sem("w_high"), sem("setup_done")
        stats_done, moments_done, var_done, rstd_done, shift_done = (
            sem("stats_done"), sem("moments_done"), sem("var_done"), sem("rstd_done"), sem("shift_done"))
        h_done, h_hi_done, h_lo_done = sem("h_done"), sem("h_hi_done"), sem("h_lo_done")
        turned, ht_hi_done, ht_lo_done = sem("turned"), sem("ht_hi_done"), sem("ht_lo_done")
        qk_ready, qk_full_done, qk_hi_done, qk_lo_done = (
            sem("qk_ready"), sem("qk_full_done"), sem("qk_hi_done"), sem("qk_lo_done"))
        score_q_ready, max_done = sem("score_q_ready"), sem("max_done")
        max_turned, neg_max_done = sem("max_turned"), sem("neg_max_done")
        v_ready, v_done = sem("v_ready"), sem("v_done")
        banks_marked, mask_laid = sem("banks_marked"), sem("mask_laid")
        score_k_ready, prob_done = sem("score_k_ready"), sem("prob_done")
        half_done, sum_done = sem("half_done"), sem("sum_done")
        pv_done, denom_ready = sem("pv_done"), sem("denom_ready")
        raw_done, recip_done, heads_done = sem("raw_done"), sem("recip_done"), sem("heads_done")
        proj_ready, proj_done = sem("proj_ready"), sem("proj_done")
        res_biased, res_added = sem("res_biased"), sem("res_added")
        o_stats_done, o_moments_done, o_var_done, o_rstd_done = (
            sem("o_stats_done"), sem("o_moments_done"), sem("o_var_done"), sem("o_rstd_done"))
        scaled_done, result_done = sem("scaled_done"), sem("result_done")

        block = ctx.enter_context(nc.Block())

        @block.sync
        def _(sp):
            sp.dma_start(adj_in, adj.rearrange("(t p) n -> p t n", p=PARTS)).then_inc(adj_loaded, 16)
            for n in range(2):
                sp.dma_start(w_in[n], w_qkv[n].rearrange("(h p) n -> p h n", p=PARTS)).then_inc(w_loaded, 16)
            for n, b_out in enumerate((b_out0, b_out1)):
                sp.dma_start(w_o[n][:], w_out[n].rearrange("(h p) n -> p h n", p=PARTS)).then_inc(consts_loaded, 16)
                sp.dma_start(bias_o[n][:], b_out.partition_broadcast(PARTS)).then_inc(consts_loaded, 16)
            sp.dma_start(bias_v[:], b_v1.partition_broadcast(PARTS)).then_inc(consts_loaded, 16)
            sp.dma_start(gamma_b[:], gamma.partition_broadcast(PARTS)).then_inc(consts_loaded, 16)
            sp.dma_start(beta_b[:], beta.partition_broadcast(PARTS)).then_inc(consts_loaded, 16)
            for n, b in enumerate((b_q1, b_k1)):
                sp.dma_start(bias_qk[:, 2 * n:2 * n + 2], b).then_inc(consts_loaded, 16)

            def stack_pair(t, d, j):
                rows = slice(HEAD * j, HEAD * (j + 1))
                for n, part in enumerate((qk_hi, qk_lo, qk_hi)):
                    sp.dma_start(q_stack[t.parity(d)][HEAD * n:HEAD * (n + 1), 2 * j:2 * j + 2, :],
                                 part[rows, 0:2, :]).then_inc(pair_stacked[j], 16)
                for n, part in enumerate((qk_hi, qk_hi, qk_lo)):
                    sp.dma_start(k_stack[t.parity(d)][HEAD * n:HEAD * (n + 1), 2 * j:2 * j + 2, :],
                                 part[rows, 2:4, :]).then_inc(pair_stacked[j], 16)

            def place_max(t, d, g):
                dst = q_stack[t.parity(d)][STACK:STACK + 1, 4 * g:4 * g + 4, :]
                sp.dma_start(dst.rearrange("o h (t n) -> o (h t) n", n=PARTS),
                             neg_max[:, :]).then_inc(max_placed[g], 16)

            def load_residual(t):
                need(sp, stored, t.count(16, -1))
                b = t.unit(-1) - BATCH * t.layer(-1)
                src = x1 if t.layer(-1) else x
                sp.dma_start(x_res[:], tokens(src, b)).then_inc(res_loaded, 16)

            def store_result(t, d):
                need(sp, result_done, t.count(1, d + 1))
                b = t.unit(d) - BATCH * t.layer(d)
                dst = out if t.layer(d) else x1
                sp.dma_start(tokens(dst, b), x_res[:]).then_inc(stored, 16)

            def step(t):
                if t.has(3):
                    need(sp, h_done, t.count(1, 3))
                    src = x1 if t.layer(3) else x
                    b = t.unit(3) - BATCH * t.layer(3)
                    sp.dma_start(x_in[:], tokens(src, b)).then_inc(x_loaded, 16)
                if t.has(1):
                    need(sp, score_k_ready, t.count(32, 0))
                    stack_pair(t, 1, PAIRS - 1)
                if t.has(0):
                    need(sp, neg_max_done, t.count(2, 1))
                    place_max(t, 0, 1)
                if t.has(-1) and t.layer(-1) and t.layer(-2):
                    load_residual(t)
                if t.has(1):
                    need(sp, neg_max_done, t.count(2, 1, 1))
                    place_max(t, 1, 0)
                change = t.has(-1) and t.layer(-1) and t.layer(-2) == 0
                if change:
                    store_result(t, -2)
                    load_residual(t)
                if t.has(2):
                    need(sp, qk_lo_done, t.count(4, 3))
                    for j in range(PAIRS - 1):
                        if j == 2 and t.has(0):
                            need(sp, score_k_ready, t.count(32, 0, 24))
                        stack_pair(t, 2, j)
                if t.has(-2) and t.layer(-2) == 0 and not change:
                    store_result(t, -2)
                if t.has(-1) and t.layer(-1) == 0:
                    load_residual(t)
                if t.has(-1) and t.layer(-1):
                    store_result(t, -1)

            run_steps(sp, step, BATCH - 4)
            sp.wait_ge(stored, 16 * UNITS)

        @block.gpsimd
        def _(pool):
            for n, m in enumerate((ident_f, ident_b, ident_h)):
                pool.memset(m[:], 0.0).then_inc(zeroed, 1)
            pool.memset(ones[:], 1.0).then_inc(pool_consts, 1)
            pool.memset(minus_half[:], -0.5).then_inc(pool_consts, 1)
            pool.memset(eps[:], EPS).then_inc(pool_consts, 1)
            pool.wait_ge(zeroed, 3)
            for m in (ident_f, ident_b, ident_h):
                pool.affine_select(out=m[:], in_=m[:], compare_op=ALU.not_equal, fill=1.0, base=0,
                                   pattern=[[-1, PARTS]], channel_multiplier=1).then_inc(pool_consts, 1)
            pool.wait_ge(pool_consts, 6)
            pool.wait_ge(consts_loaded, CONSTS)

            def reciprocal_root(t, var_in, var_out, root, semaphores, value):
                pool.tensor_tensor(var_out[:], var_in, eps[:], ALU.add).then_inc(semaphores[0], 1)
                pool.wait_ge(semaphores[0], value)
                pool.tensor_tensor(root[:], var_out[:], minus_half[:], ALU.pow).then_inc(semaphores[1], 1)

            def sum_head(t, h):
                need(pool, prob_done, t.count(32, 0, 4 * h + 4))
                need(pool, sum_done, t.count(8, 0, h))
                pool.tensor_tensor(half_sum[:], prob[:, h, 0:2, :], prob[:, h, 2:4, :], ALU.add).then_inc(half_done, 1)
                pool.wait_ge(half_done, t.count(8, 0, h + 1))
                need(pool, denom_ready, t.count(2, -1, h // 4 + 1))
                pool.tensor_tensor(prob_sum[:, h, :], half_sum[:, 0, :], half_sum[:, 1, :], ALU.add).then_inc(sum_done, 1)

            def bias_residual(t, d):
                need(pool, res_loaded, t.count(16, d + 1))
                for k in range(2):
                    add = twice(bias_o[1] if t.layer(d) else beta_b)
                    pool.tensor_tensor(x_res[:, 2 * k:2 * k + 2, :], x_res[:, 2 * k:2 * k + 2, :], add,
                                       ALU.add).then_inc(res_biased, 1)

            def step(t):
                for s in range(SLOTS):
                    if s == 2 and t.has(-2) and t.layer(-2) == 0:
                        bias_residual(t, -2)
                        need(pool, proj_done, t.count(2, -1))
                        need(pool, res_biased, t.count(2, -1))
                        pool.tensor_tensor(x_res[:], x_res[:], proj[:], ALU.add).then_inc(res_added, 1)
                    if s == 3 and t.has(-2) and t.layer(-2) == 0:
                        need(pool, o_moments_done, t.count(4, -1))
                        need(pool, result_done, t.count(1, -2))
                        reciprocal_root(t, o_moments[:, :, 1], o_var, o_rstd, (o_var_done, o_rstd_done), t.count(1, -1))
                    if s == 6 and t.has(3):
                        need(pool, moments_done, t.count(4, 4))
                        need(pool, h_done, t.count(1, 3))
                        reciprocal_root(t, moments[:, :, 1], var_eps, rstd, (var_done, rstd_done), t.count(1, 4))
                    if s == 6 and t.has(-1) and t.layer(-1):
                        bias_residual(t, -1)
                    if t.has(0):
                        sum_head(t, s)

            run_steps(pool, step)

        @block.scalar
        def _(act):
            def h_of(t, k):
                if k == 0:
                    need(act, shift_done, t.count(1, 3))
                    need(act, h_lo_done, t.count(2, 2))
                for n in (2 * k, 2 * k + 1):
                    last = nc.scalar.activation(h_full[:, n, :], x_in[:, n, :], ACT.Relu,
                                                bias=shift[:, n:n + 1], scale=rstd[:, n:n + 1])
                if k == 1:
                    last.then_inc(h_done, 1)

            def h_high(t, k):
                act.wait_ge(h_done, t.count(1, 3))
                need(act, turned, t.count(2, 2))
                nc.scalar.activation(h_hi[:, 2 * k:2 * k + 2, :], h_full[:, 2 * k:2 * k + 2, :], ACT.Copy
                                     ).then_inc(h_hi_done, 1)

            def qk_of(t, m):
                need(act, qk_ready, t.count(4, 2, m + 1))
                need(act, qk_lo_done, t.count(4, 2, m - 1))
                bias = bias_qk[:, m:m + 1] if t.layer(2) else 0.0
                nc.scalar.activation(qk_full[:, m % 2, :], work[QK_BANK[m]][:], ACT.Identity, bias=bias,
                                     scale=1.0 / W_SCALE).then_inc(qk_full_done, 1)
                for j in range(PAIRS):
                    need(act, pair_stacked[j], t.count(STACK_DMAS, 2))
                nc.scalar.activation(qk_hi[:, m, :], work[QK_BANK[m]][:], ACT.Identity, bias=bias,
                                     scale=1.0 / W_SCALE).then_inc(qk_hi_done, 1)

            def lay_mask(t, n):
                s, q = divmod(n, QUARTERS)
                if q < LAID:
                    need(act, prob_done, t.count(32, 0, n - 1))
                    nc.scalar.activation(score_k[q % 2][:], mask_k[:, q, :], ACT.Copy).then_inc(mask_laid, 1)

            def step(t):
                for s in range(SLOTS):
                    for q in range(QUARTERS):
                        if s == 0 and q in (0, 1) and t.has(2):
                            h_of(t, q)
                        if s == 0 and q in (2, 3) and t.has(2):
                            h_high(t, q - 2)
                        if s == 2 and q == 1 and t.has(2):
                            need(act, turned, t.count(2, 3))
                            need(act, v_ready, t.count(2, 1) if t.has(0) else 0)
                            nc.scalar.activation(ht_lo[t.parity(2)][:].rearrange("p h n -> p (h n)"),
                                                 work[0][:].bitcast(F16), ACT.Copy).then_inc(ht_lo_done, 1)
                        if 3 <= s < 3 + QK_TILES and q == 0 and t.has(2):
                            qk_of(t, s - 3)
                        if t.has(0):
                            need(act, score_k_ready, t.count(32, 0, 4 * s + q + 1))
                            if q == 0:
                                need(act, pv_done, t.count(8, -1, 4 * (s // 4 + 1)))
                                need(act, half_done, t.count(8, -1, s + 1))
                            nc.scalar.activation(prob[:, s, q, :], score_k[q % 2][:], ACT.Exp,
                                                 scale=1.0 / ROOT).then_inc(prob_done, 1)
                        n = 4 * s + q + 2
                        if n < 32 and t.has(0):
                            lay_mask(t, n)
                        if n >= 32 and t.has(1):
                            lay_mask(t.next(), n - 32)
                        if q == 3 and ((s == 3 and t.has(-1)) or (s == 7 and t.has(0))):
                            done = t.count(2, 0) if s == 3 else t.count(2, 0, 1)
                            need(act, pv_done, t.count(8, 0) if s == 3 else t.count(8, 0, 4))
                            need(act, heads_done, done - 1)
                            nc.scalar.activation(heads_raw[:], pv[:], ACT.Copy).then_inc(raw_done, 1)

            act.wait_ge(setup_done, 6)
            act.wait_ge(banks_marked, 1)
            run_steps(act, step)

        @block.vector
        def _(dve):
            tiles_asked = dve.alloc_register("tiles_asked")
            dve.reg_mov(tiles_asked, 0)
            for n in range(2):
                nc.vector.memset(k_stack[n][STACK:STACK + 1, :, :], 1.0).then_inc(setup_done, 1)
            dve.wait_ge(adj_loaded, 16)
            nc.vector.tensor_scalar(mask_q[:], adj_in, 0.0, MASKED, ALU.is_equal, ALU.mult).then_inc(mask_made, 1)
            dve.wait_ge(w_loaded, 32)
            for n in range(2):
                nc.vector.tensor_scalar(w_hi[n][:], w_in[n], W_SCALE, None, ALU.mult).then_inc(w_high, 1)
                dve.wait_ge(w_high, n + 1)
                nc.vector.scalar_tensor_tensor(
                    w_lo[n][:].rearrange("p h n -> p (h n)"), w_in[n].rearrange("p h n -> p (h n)"), W_SCALE,
                    w_hi[n][:].rearrange("p h n -> p (h n)"), ALU.mult, ALU.subtract).then_inc(setup_done, 1)
            for n in range(2):
                dve.wait_ge(mask_turned, n + 1)
                nc.vector.tensor_copy(mask_k[:, 2 * n:2 * n + 2, :].rearrange("p t n -> p (t n)"),
                                      work[n][:].bitcast(BF16)).then_inc(setup_done, 1)
            dve.wait_ge(setup_done, 6)
            dve.wait_ge(consts_loaded, CONSTS)
            dve.wait_ge(pool_consts, 6)

            def tile_stats(t, source, st, semaphore, k):
                for n in (2 * k, 2 * k + 1):
                    nc.vector.bn_stats(st[:, n, :], source[:, n, :]).then_inc(semaphore, 1)

            def tile_moments(t, st, mom, semaphores, value):
                dve.wait_ge(semaphores[0], value)
                nc.vector.memset(flag[:], 0.0)
                for n in range(TILES):
                    nc.vector.bn_aggr(mom[:, n, :], st[:, n, :]).then_inc(semaphores[1], 1)

            def max_of(t, s, q):
                if q == 0 and s % 4 == 0:
                    need(dve, max_turned, t.count(2, 0, s // 4 + 1))
                dve.reg_add(tiles_asked, tiles_asked, 1)
                dve.wait_ge(setup_done, 6)
                dve.wait_ge(score_q_ready, tiles_asked)
                nc.vector.tensor_tensor_reduce(out=unused[:, q % 2, :], in0=score_q[q % 2][:], in1=mask_q[:, q, :],
                                               scale=1.0, scalar=-3.0e38, op0=ALU.add, op1=ALU.max,
                                               accum_out=row_max[:, s, q:q + 1]).then_inc(max_done, 1)

            def negate_max(t, d, g):
                need(dve, max_turned, t.count(2, d, g + 1))
                need(dve, max_placed[1 - g], t.count(16, d, 16 * g))
                nc.vector.tensor_scalar(neg_max[:], work[1 - g][0:4 * TILES, 0:PARTS], -1.0, None,
                                        ALU.mult).then_inc(neg_max_done, 1)

            def reciprocals(t, d, g, k):
                if k == 0:
                    need(dve, denom_ready, t.count(2, d, g + 1))
                    need(dve, heads_done, t.count(2, d, g))
                columns = slice(PARTS * k, PARTS * (k + 1))
                nc.vector.reciprocal(recip[:, columns], denom[:, columns]).then_inc(recip_done, 1)

            def normalise(t, d, g):
                need(dve, recip_done, t.count(8, d, 4 * (g + 1)))
                need(dve, raw_done, t.count(2, d, g + 1))
                need(dve, proj_ready, t.count(2, d))
                nc.vector.tensor_tensor(heads_t[:, g, :], heads_raw[:], recip[:], ALU.mult).then_inc(heads_done, 1)

            def take_v(t, k):
                need(dve, v_ready, t.count(2, 0, k + 1))
                need(dve, pv_done, t.count(8, -1))
                dst = v[t.parity(0)][:, 2 * k:2 * k + 2, :]
                bank = work[1 - k][:].rearrange("p (t n) -> p t n", t=2)
                if t.layer(0):
                    nc.vector.scalar_tensor_tensor(dst, bank, 1.0 / W_SCALE, twice(bias_v),
                                                   ALU.mult, ALU.add).then_inc(v_done, 1)
                else:
                    nc.vector.tensor_scalar(dst, bank, 1.0 / W_SCALE, None, ALU.mult).then_inc(v_done, 1)

            def take_projection(t, k):
                need(dve, proj_ready, t.count(2, -1, k + 1))
                tiles = slice(2 * k, 2 * k + 2)
                bank = work[1 - k][:].rearrange("p (t n) -> p t n", t=2)
                if t.layer(-1):
                    need(dve, res_biased, t.count(2, -1, k + 1))
                    nc.vector.tensor_tensor(x_res[:, tiles, :], bank, x_res[:, tiles, :], ALU.add
                                            ).then_inc(proj_done, 1)
                    if k == 1:
                        need(dve, proj_done, t.count(2, 0))
                        nc.vector.memset(flag[:], 0.0).then_inc(result_done, 1)
                else:
                    need(dve, result_done, t.count(1, -1))
                    nc.vector.tensor_tensor(proj[:, tiles, :], bank, twice(bias_o[0]), ALU.add).then_inc(proj_done, 1)

            def scale_0(t, k):
                need(dve, res_added, t.count(1, -1))
                for n in (2 * k, 2 * k + 1):
                    nc.vector.scalar_tensor_tensor(proj[:, n, :], proj[:, n, :], o_moments[:, n, 0:1], gamma_b[:],
                                                   ALU.subtract, ALU.mult).then_inc(scaled_done, 1)

            def finish_0(t, k):
                need(dve, o_rstd_done, t.count(1, -1))
                for n in (2 * k, 2 * k + 1):
                    need(dve, scaled_done, t.count(4, -2, n + 1))
                    last = nc.vector.scalar_tensor_tensor(x_res[:, n, :], proj[:, n, :], o_rstd[:, n:n + 1],
                                                          x_res[:, n, :], ALU.mult, ALU.add)
                if k == 1:
                    last.then_inc(result_done, 1)

            def work_of(t, s, q):
                at = (s, q)
                finishing = t.has(-2) and t.layer(-2) == 0
                if at == (0, 0) and finishing:
                    need(dve, proj_done, t.count(2, -1))
                    need(dve, o_moments_done, t.count(4, -2))
                    tile_stats(t, proj, o_stats, o_stats_done, 0)
                if at == (0, 1) and finishing:
                    tile_stats(t, proj, o_stats, o_stats_done, 1)
                if at == (0, 2) and t.has(0):
                    negate_max(t, 0, 1)
                if at in ((0, 3), (1, 1)) and t.has(2):
                    k = s
                    need(dve, h_hi_done, t.count(2, 2, k + 1))
                    need(dve, turned, t.count(2, 2))
                    tiles = slice(2 * k, 2 * k + 2)
                    nc.vector.tensor_tensor(h_lo[:, tiles, :], h_full[:, tiles, :], h_hi[:, tiles, :], ALU.subtract
                                            ).then_inc(h_lo_done, 1)
                if at == (1, 0) and t.has(0):
                    take_v(t, 0)
                if at == (1, 2) and t.has(0):
                    take_v(t, 1)
                if at == (3, 1) and finishing:
                    need(dve, scaled_done, t.count(4, -2))
                    need(dve, o_rstd_done, t.count(1, -2))
                    tile_moments(t, o_stats, o_moments, (o_stats_done, o_moments_done), t.count(4, -1))
                if at in ((2, 0), (2, 1)) and t.has(2):
                    need(dve, turned, t.count(2, 2, 1))
                    need(dve, v_ready, t.count(2, 1) if t.has(0) else 0)
                    nc.vector.tensor_copy(ht_hi[t.parity(2)][:, q, :],
                                          work[1][:].bitcast(F16).rearrange("p (h n) -> p h n", h=HALVES)[:, q, :]
                                          ).then_inc(ht_hi_done, 1)
                for k, place in enumerate(((1, 3), (2, 2), (2, 3), (3, 0))):
                    if at == place and t.has(-1):
                        reciprocals(t, -1, 0, k)
                if 3 <= s < 3 + QK_TILES and q == 2 and t.has(2):
                    m = s - 3
                    need(dve, qk_hi_done, t.count(4, 2, m + 1))
                    for j in range(PAIRS):
                        need(dve, pair_stacked[j], t.count(STACK_DMAS, 2))
                    nc.vector.tensor_tensor(qk_lo[:, m, :], qk_full[:, m % 2, :], qk_hi[:, m, :],
                                            ALU.subtract).then_inc(qk_lo_done, 1)
                if at == (3, 3) and t.has(-1):
                    normalise(t, -1, 0)
                if at == (4, 0) and t.has(3):
                    need(dve, x_loaded, t.count(16, 4))
                    need(dve, moments_done, t.count(4, 3))
                    tile_stats(t, x_in, stats, stats_done, 0)
                if at == (4, 1) and t.has(3):
                    tile_stats(t, x_in, stats, stats_done, 1)
                if at == (4, 2) and t.has(1):
                    negate_max(t, 1, 0)
                for k, place in enumerate(((4, 3), (5, 0), (5, 1), (5, 3))):
                    if at == place and t.has(-1):
                        reciprocals(t, -1, 1, k)
                if at == (5, 2) and t.has(3):
                    need(dve, shift_done, t.count(1, 3))
                    tile_moments(t, stats, moments, (stats_done, moments_done), t.count(4, 4))
                if at == (6, 0) and t.has(-1):
                    normalise(t, -1, 1)
                last = t.i is None and t.c == BATCH + 1
                places = ((4, 3), (5, 0), (5, 1), (5, 2)) if last else ((6, 1), (6, 3), (7, 0), (7, 1))
                for k, place in enumerate(places):
                    if at == place and finishing:
                        scale_0(t, k) if k < 2 else finish_0(t, k - 2)
                if at == (7, 2) and t.has(-1):
                    take_projection(t, 0)
                if at == (7, 3) and t.has(3):
                    need(dve, rstd_done, t.count(1, 4))
                    nc.vector.scalar_tensor_tensor(shift[:], moments[:, :, 0], -1.0, rstd[:],
                                                   ALU.mult, ALU.mult).then_inc(shift_done, 1)

            def step(t):
                for s in range(SLOTS):
                    for q in range(QUARTERS):
                        if t.has(1):
                            max_of(t, s, q)
                        work_of(t, s, q)
                if t.has(-1):
                    take_projection(t, 1)

            run_steps(dve, step)

        @block.tensor
        def _(pe):
            pe.wait_ge(pool_consts, 6)
            pe.wait_ge(mask_made, 1)
            for n in range(2):
                turned_mask = work[n][:].bitcast(BF16).rearrange("p (t n) -> p t n", t=2)
                for k in range(2):
                    for q in range(TILES):
                        key = PARTS * (2 * n + k)
                        last = nc.tensor.transpose(turned_mask[:, k, PARTS * q:PARTS * (q + 1)],
                                                   mask_q[:, q, key:key + PARTS], ident_b[:])
                last.then_inc(mask_turned, 1)
            pe.wait_ge(setup_done, 6)
            pe.wait_ge(consts_loaded, CONSTS)
            for bank in score_k:
                last = nc.tensor.matmul(bank[:], ident_b[:], mask_k[:, 0, :], start=True, stop=True)
            last.then_inc(banks_marked, 1)

            def scores_by_key(t, s, q):
                if s % 4 == 0 and q == 0:
                    need(pe, max_placed[s // 4], t.count(16, 1))
                bank = score_k[q % 2]
                if q < LAID:
                    need(pe, mask_laid, t.count(LAID * SLOTS, 0, LAID * s + q + 1))
                else:
                    need(pe, prob_done, t.count(32, 0, 4 * s + q - 1))
                    nc.tensor.matmul(bank[:], ident_b[:], mask_k[:, q, :], start=True, stop=False)
                nc.tensor.matmul(bank[:], k_stack[t.parity(0)][0:STACK + 1, s, PARTS * q:PARTS * (q + 1)],
                                 q_stack[t.parity(0)][0:STACK + 1, s, :], start=False, stop=True,
                                 skip_group_check=q < LAID).then_inc(score_k_ready, 1)

            def scores_by_query(t, s, q):
                if s % 2 == 0 and q == 0:
                    need(pe, pair_stacked[s // 2], t.count(STACK_DMAS, 2))
                need(pe, max_done, t.count(32, 1, 4 * s + q - 1))
                nc.tensor.matmul(score_q[q % 2][:], q_stack[t.parity(1)][0:STACK, s, PARTS * q:PARTS * (q + 1)],
                                 k_stack[t.parity(1)][0:STACK, s, :], start=True, stop=True
                                 ).then_inc(score_q_ready, 1)

            def times_v(t, d, g, k):
                if k == 0:
                    need(pe, prob_done, t.count(32, d, 16 * (g + 1)))
                    need(pe, v_done, t.count(2, d + 1))
                    need(pe, raw_done, t.count(2, d, g))
                for j in range(4):
                    h = 4 * g + j
                    last = nc.tensor.matmul(pv[HEAD * j:HEAD * (j + 1), :], v[t.parity(d)][:, k, HEAD * h:HEAD * (h + 1)],
                                            prob[:, h, k, :], start=(k == 0), stop=(k == TILES - 1))
                last.then_inc(pv_done, 1)

            def sum_rows(t, d, g):
                need(pe, sum_done, t.count(8, d, 4 * (g + 1)))
                need(pe, recip_done, t.count(8, d, 4 * g))
                for j in range(4):
                    last = nc.tensor.matmul(denom[HEAD * j:HEAD * (j + 1), :], ones[:], prob_sum[:, 4 * g + j, :],
                                            start=True, stop=True)
                last.then_inc(denom_ready, 1)

            def turn_h(t, part, bank):
                dst = work[bank][:].bitcast(F16).rearrange("p (h n) -> p h n", h=HALVES)
                for k in range(HALVES):
                    for n in range(TILES):
                        last = nc.tensor.transpose(dst[:, k, PARTS * n:PARTS * (n + 1)],
                                                   part[:, n, PARTS * k:PARTS * (k + 1)], ident_h[:])
                last.then_inc(turned, 1)

            def qk_terms(t):
                hi, lo = w_hi[t.layer(2)], w_lo[t.layer(2)]
                p = t.parity(2)
                return [(w, ht, k) for w, ht in ((hi, ht_hi[p]), (lo, ht_hi[p]), (hi, ht_lo[p])) for k in range(HALVES)]

            def project_qk(t, m, part):
                terms = qk_terms(t)
                for n in range(3 * part, 3 * part + 3):
                    w, ht, k = terms[n]
                    last = nc.tensor.matmul(work[QK_BANK[m]][:], w[:, k, PARTS * m:PARTS * (m + 1)], ht[:, k, :],
                                            start=(n == 0), stop=(n == 5))
                if part == 1:
                    last.then_inc(qk_ready, 1)

            def project_v(t, n):
                hi, lo = w_hi[t.layer(0)], w_lo[t.layer(0)]
                p = t.parity(0)
                terms = [(w, ht, k) for w, ht in ((hi, ht_hi[p]), (lo, ht_hi[p]), (hi, ht_lo[p])) for k in range(HALVES)]
                dst = work[1 - n // 2][:].rearrange("p (t n) -> p t n", t=2)[:, n % 2, :]
                for i, (w, ht, k) in enumerate(terms):
                    last = nc.tensor.matmul(dst, ht[:, k, PARTS * n:PARTS * (n + 1)], w[:, k, 2 * DIM:3 * DIM],
                                            start=(i == 0), stop=(i == 5))
                if n % 2:
                    last.then_inc(v_ready, 1)

            def turn_max(t, d, g):
                need(pe, max_done, t.count(32, d, 16 * (g + 1)))
                nc.tensor.matmul(work[1 - g][0:4 * TILES, 0:PARTS],
                                 row_max[:, 4 * g:4 * g + 4, :].rearrange("p h t -> p (h t)"), ident_f[:],
                                 start=True, stop=True).then_inc(max_turned, 1)

            def project_out(t, n):
                dst = work[1 - n // 2][:].rearrange("p (t n) -> p t n", t=2)[:, n % 2, :]
                for half in range(HALVES):
                    last = nc.tensor.matmul(dst, heads_t[:, half, PARTS * n:PARTS * (n + 1)],
                                            w_o[t.layer(-1)][:, half, :], start=(half == 0), stop=(half == 1))
                if n % 2:
                    last.then_inc(proj_ready, 1)

            def banks_free(t):
                for semaphore, per, d, extra in ((ht_hi_done, 2, 2, 0), (ht_lo_done, 1, 2, 0), (qk_hi_done, 4, 2, 0),
                                                 (v_done, 2, 0, 0), (neg_max_done, 2, 0, 1), (proj_done, 2, -1, 0)):
                    need(pe, semaphore, min(t.count(per, d, extra), per * UNITS))

            def step(t):
                if t.i is None and (t.c < 2 or t.c > UNITS - 4):
                    banks_free(t)
                for s in range(SLOTS):
                    for q in range(QUARTERS):
                        if t.has(0):
                            scores_by_key(t, s, q)
                        if t.has(1):
                            scores_by_query(t, s, q)
                        if q == 1 and s < 4 and t.has(-1):
                            times_v(t, -1, 1, s)
                        if q == 1 and s >= 4 and t.has(0):
                            times_v(t, 0, 0, s - 4)
                        if (s, q) == (4, 0) and t.has(-1):
                            sum_rows(t, -1, 1)
                        if (s, q) == (7, 3) and t.has(0):
                            sum_rows(t, 0, 0)
                        if (s, q) == (0, 0) and t.has(0):
                            need(pe, proj_done, t.count(2, -1, -1))
                            project_v(t, 0)
                        if (s, q) == (0, 1) and t.has(0):
                            need(pe, proj_done, t.count(2, -1))
                            turn_max(t, 0, 1)
                        if (s, q) == (0, 2) and t.has(0):
                            project_v(t, 1)
                        if (s, q) == (0, 3) and t.has(0):
                            need(pe, neg_max_done, t.count(2, 1))
                            project_v(t, 2)
                        if (s, q) == (1, 0) and t.has(0):
                            project_v(t, 3)
                        if (s, q) == (1, 2) and t.has(2):
                            need(pe, h_hi_done, t.count(2, 3))
                            need(pe, v_done, t.count(2, 0, 1))
                            turn_h(t, h_hi, 1)
                        if (s, q) == (2, 0) and t.has(2):
                            need(pe, h_lo_done, t.count(2, 3))
                            need(pe, v_done, t.count(2, 1) if t.has(0) else 0)
                            turn_h(t, h_lo, 0)
                        if 2 <= s < 2 + QK_TILES and q in (2, 3) and t.has(2):
                            m = s - 2
                            if m == 0:
                                if q == 2:
                                    need(pe, ht_hi_done, t.count(2, 3))
                                else:
                                    need(pe, ht_lo_done, t.count(1, 3))
                            elif q == 2:
                                need(pe, qk_hi_done, t.count(4, 2, m))
                            project_qk(t, m, q - 2)
                        if (s, q) == (4, 1) and t.has(1):
                            if t.has(2):
                                need(pe, qk_hi_done, t.count(4, 2, 1))
                            else:
                                need(pe, v_done, t.count(2, 1))
                            turn_max(t, 1, 0)
                        if (s, q) in ((6, 2), (6, 3), (7, 0), (7, 2)) and t.has(-1):
                            n = ((6, 2), (6, 3), (7, 0), (7, 2)).index((s, q))
                            if n == 0:
                                need(pe, heads_done, t.count(2, 0))
                                if t.has(1):
                                    need(pe, neg_max_done, t.count(2, 1, 1))
                                elif t.has(0):
                                    need(pe, v_done, t.count(2, 1))
                            if n == 2:
                                if t.has(2):
                                    need(pe, qk_hi_done, t.count(4, 3))
                                elif t.has(0):
                                    need(pe, v_done, t.count(2, 1))
                            project_out(t, n)

            run_steps(pe, step)


def kernel(**inputs):
    import numpy as np
    import concourse.bacc as bacc
    from concourse import mybir
    from concourse.bass_utils import run_bass_kernel_spmd

    def even_odd(w):
        return np.concatenate([w.reshape(DIM, PAIRS, 2, HEAD)[:, :, g, :].reshape(DIM, -1) for g in range(2)], 1)

    def by_head_tile(b):
        return np.ascontiguousarray(b.reshape(PAIRS, 2, HEAD).transpose(0, 2, 1).reshape(-1, 2))

    a = {name: np.asarray(value) for name, value in inputs.items()}
    w0 = a["L0_gnn_w_qkv"]
    arrays = {
        "x": a["x"], "adj": a["adj"],
        "w_qkv0": np.concatenate([even_odd(w0[:, :DIM]), even_odd(w0[:, DIM:2 * DIM]), w0[:, 2 * DIM:]], 1),
        "w_out0": a["L0_gnn_w_proj"], "b_out0": a["L0_gnn_b_proj"],
        "gamma": a["L0_gnn_ln_gamma"], "beta": a["L0_gnn_ln_beta"],
        "w_qkv1": np.concatenate([even_odd(a["L1_gnn_Wq"]), even_odd(a["L1_gnn_Wk"]), a["L1_gnn_Wv"]], 1),
        "b_q1": by_head_tile(a["L1_gnn_bq"]), "b_k1": by_head_tile(a["L1_gnn_bk"]), "b_v1": a["L1_gnn_bv"],
        "w_out1": a["L1_gnn_Wo"], "b_out1": a["L1_gnn_bo"],
    }
    nc = bacc.Bacc("TRN2", target_bir_lowering=False, num_devices=1)
    args = {}
    for name, value in arrays.items():
        arrays[name] = np.ascontiguousarray(value)
        args[name] = nc.dram_tensor(name, value.shape, mybir.dt.from_np(value.dtype), kind="ExternalInput").ap()
    out = nc.dram_tensor("out", (BATCH, TOKENS, DIM), mybir.dt.float32, kind="ExternalOutput").ap()
    build(nc, out=out, **args)
    r = run_bass_kernel_spmd(nc, [arrays], core_ids=[0])
    return r.results[0]["out"]
```

```python
import concourse.bass as bass
from concourse import mybir
from contextlib import ExitStack

F32, F16, BF16 = mybir.dt.float32, mybir.dt.float16, mybir.dt.bfloat16
ALU, ACT = mybir.AluOpType, mybir.ActivationFunctionType

PARTS = 128
BATCH, TOKENS, DIM, HEADS = 16, 512, 256, 8
HEAD = DIM // HEADS
UNITS = 2 * BATCH
TILES = TOKENS // PARTS
HALVES = DIM // PARTS
SLOTS, QUARTERS = HEADS, TILES
PAIRS = HEADS // 2
QK_TILES = 4
STACK = 3 * HEAD
W_SCALE = 256.0
ROOT = float(HEAD) ** 0.5
MASKED = -1.0e9 * ROOT
EPS = 1e-5
CONSTS = 16 * 9
QK_AT = ((2, 2), (2, 2), (3, 2), (3, 3), (4, 2), (4, 3), (5, 2), (5, 3))
K_BANKS = 3
LAID_BY = "STTSTSTS" "STTSSSSS"
POOL_CONSTS = 7
STACK_DMAS = 3 * 16


def twice(row):
    return row[:, :].unsqueeze(1).to_broadcast([PARTS, 2, DIM])


class Step:

    def __init__(self, c, i=None, layers=None):
        self.c, self.i, self.layers = c, i, layers

    def has(self, d):
        return self.i is not None or 0 <= self.c + d < UNITS

    def layer(self, d):
        return self.layers if self.i is not None else (self.c + d) // BATCH

    def parity(self, d):
        return (self.c + d) % 2

    def count(self, per_unit, d, extra=0):
        least = per_unit * (self.c + d) + extra
        return least if self.i is None else self.i * (2 * per_unit) + least

    def next(self):
        return Step(self.c + 1, self.i, self.layers)

    def unit(self, d):
        return self.c + d if self.i is None else self.i * 2 + (self.c + d)


def by_vector(t, h):
    return t.i is None and t.c == UNITS - 1 and h >= 4


def qk_bank(t, m):
    return m % 2 if t.i is None and t.c == -2 else 0


def laid_by(n):
    return {"S": "scalar", "T": "tensor"}[LAID_BY[n % len(LAID_BY)]]


def exp_before(t, n):
    if n >= K_BANKS:
        return t.count(32, 0, n - K_BANKS + 1)
    return t.count(32, 0, {0: -1, 1: 0, 2: 0}[n])


def need(engine, semaphore, value):
    if not isinstance(value, int) or value > 0:
        engine.wait_ge(semaphore, value)


def run_steps(engine, step, change=14):
    for t in range(-1, 2):
        step(Step(t))
    with engine.Fori(1, change // 2) as i:
        step(Step(0, i, 0))
        step(Step(1, i, 0))
    for t in range(change, 18):
        step(Step(t))
    with engine.Fori(9, 14) as i:
        step(Step(0, i, 1))
        step(Step(1, i, 1))
    for t in range(28, UNITS + 1):
        step(Step(t))


def build(nc, x, adj, w_qkv0, w_out0, b_out0, gamma, beta, w_qkv1, b_q1, b_k1, b_v1, w_out1, b_out1, out):
    x1 = nc.dram_tensor("x1", [BATCH, TOKENS, DIM], F32).ap()
    recip_rows = nc.dram_tensor("recip_rows", [HEADS, TOKENS], F32).ap()
    w_qkv, w_out = (w_qkv0, w_qkv1), (w_out0, w_out1)

    def tokens(a, b):
        return a.rearrange("b (t p) d -> p b t d", p=PARTS)[:, bass.ds(b, 1), :, :].rearrange("p b t d -> p (b t) d")

    with ExitStack() as ctx:
        def sb(name, shape, dt):
            return ctx.enter_context(nc.sbuf_tensor(name, shape, dt))

        def ps(name):
            return ctx.enter_context(nc.psum_tensor(name, [PARTS, 512], F32))

        def sem(name):
            return ctx.enter_context(nc.semaphore(name))

        ident_f = sb("ident_f", [PARTS, PARTS], F32)
        ident_b = sb("ident_b", [PARTS, PARTS], BF16)
        ident_h = sb("ident_h", [PARTS, PARTS], F16)
        pick = sb("pick", [PARTS, 2, HEAD], F32)
        eps = sb("eps", [PARTS, TILES], F32)
        minus_half = sb("minus_half", [PARTS, TILES], F32)
        mask_q = sb("mask_q", [PARTS, TILES, TOKENS], BF16)
        mask_k = sb("mask_k", [PARTS, TILES, TOKENS], BF16)
        w_hi = [sb(f"w_hi{n}", [PARTS, HALVES, 3 * DIM], F16) for n in range(2)]
        w_lo = [sb(f"w_lo{n}", [PARTS, HALVES, 3 * DIM], F16) for n in range(2)]
        w_o = [sb(f"w_o{n}", [PARTS, HALVES, DIM], F32) for n in range(2)]
        bias_o = [sb(f"bias_o{n}", [PARTS, DIM], F32) for n in range(2)]
        bias_v = sb("bias_v", [PARTS, DIM], F32)
        bias_qk = sb("bias_qk", [PARTS, QK_TILES], F32)
        gamma_b = sb("gamma_b", [PARTS, DIM], F32)
        beta_b = sb("beta_b", [PARTS, DIM], F32)
        flag = sb("flag", [1, 1], F32)
        x_in = sb("x_in", [PARTS, TILES, DIM], F32)
        stats = sb("stats", [PARTS, TILES, 6], F32)
        moments = sb("moments", [PARTS, TILES, 2], F32)
        var_eps = sb("var_eps", [PARTS, TILES], F32)
        rstd = sb("rstd", [PARTS, TILES], F32)
        shift = sb("shift", [PARTS, TILES], F32)
        h_full = sb("h_full", [PARTS, TILES, DIM], F32)
        h_hi = sb("h_hi", [PARTS, TILES, DIM], F16)
        h_lo = sb("h_lo", [PARTS, TILES, DIM], F16)
        ht_hi = [sb(f"ht_hi{n}", [PARTS, HALVES, TOKENS], F16) for n in range(2)]
        ht_lo = [sb(f"ht_lo{n}", [PARTS, HALVES, TOKENS], F16) for n in range(2)]
        qk_full = sb("qk_full", [PARTS, 2, TOKENS], F32)
        qk_parts = sb("qk_parts", [PARTS, 4, 2, TOKENS], F16)
        stack = [sb(f"stack{n}", [PARTS, 2, HEADS, TOKENS], F16) for n in range(2)]
        q_stack, k_stack = ([both[:, n, :, :] for both in stack] for n in range(2))

        def high(m):
            return qk_parts[:, 2 * (m // 2), m % 2, :]

        def low(m):
            return qk_parts[:, 2 * (m // 2) + 1, m % 2, :]

        unused = sb("unused", [PARTS, 2, TOKENS], BF16)
        row_max = sb("row_max", [PARTS, HEADS, TILES], F32)
        neg_max = sb("neg_max", [4 * TILES, PARTS], F16)
        v = [sb(f"v{n}", [PARTS, TILES, DIM], F32) for n in range(2)]
        prob = sb("prob", [PARTS, HEADS, TILES, TOKENS], F32)
        half_sum = sb("half_sum", [PARTS, 2, TOKENS], F32)
        prob_sum = sb("prob_sum", [PARTS, HEADS, TOKENS], F32)
        recip = [sb(f"recip{g}", [PARTS, TOKENS], F32) for g in range(2)]
        sums = sb("sums", [PARTS, HEADS * TOKENS // PARTS], F32)
        heads_t = sb("heads_t", [PARTS, 2, TOKENS], F32)
        x_res = sb("x_res", [PARTS, TILES, DIM], F32)
        proj = sb("proj", [PARTS, TILES, DIM], F32)
        o_stats = sb("o_stats", [PARTS, TILES, 6], F32)
        o_moments = sb("o_moments", [PARTS, TILES, 2], F32)
        o_var = sb("o_var", [PARTS, TILES], F32)
        o_rstd = sb("o_rstd", [PARTS, TILES], F32)

        staging = prob[:, :, :, :].rearrange("p h k n -> p (h k n)")
        adj_in = staging[:, 0:TILES * TOKENS].rearrange("p (t n) -> p t n", t=TILES)
        W = HALVES * 3 * DIM
        w_in = [staging[:, 2048 + n * W:2048 + (n + 1) * W].rearrange("p (h n) -> p h n", h=HALVES)
                for n in range(2)]

        score_k = [ps(f"score_k{n}") for n in range(K_BANKS)]
        score_q = [ps(f"score_q{n}") for n in range(2)]
        pv = ps("pv")
        work = [ps(f"work{n}") for n in range(2)]

        adj_loaded, consts_loaded = sem("adj_loaded"), sem("consts_loaded")
        w_loaded = [sem(f"w_loaded{n}") for n in range(2)]
        x_loaded = sem("x_loaded")
        res_loaded = sem("res_loaded")
        stored = sem("stored")
        pair_stacked = [sem(f"pair_stacked{j}") for j in range(PAIRS)]
        max_placed = [sem(f"max_placed{g}") for g in range(2)]
        zeroed, pool_consts, mask_made, mask_turned = (
            sem("zeroed"), sem("pool_consts"), sem("mask_made"), sem("mask_turned"))
        w_high, w_split = sem("w_high"), sem("w_split")
        mask_k_done, row_set = sem("mask_k_done"), sem("row_set")
        stats_done, moments_done, var_done, rstd_done, shift_done = (
            sem("stats_done"), sem("moments_done"), sem("var_done"), sem("rstd_done"), sem("shift_done"))
        h_done, h_hi_done, h_lo_done = sem("h_done"), sem("h_hi_done"), sem("h_lo_done")
        turned, ht_hi_done, ht_lo_done = sem("turned"), sem("ht_hi_done"), sem("ht_lo_done")
        qk_ready, qk_full_done, qk_hi_done, qk_lo_done = (
            sem("qk_ready"), sem("qk_full_done"), sem("qk_hi_done"), sem("qk_lo_done"))
        score_q_ready, max_done = sem("score_q_ready"), sem("max_done")
        max_turned, neg_max_done = sem("max_turned"), sem("neg_max_done")
        v_ready, v_done = sem("v_ready"), sem("v_done")
        banks_marked = sem("banks_marked")
        mask_laid = sem("mask_laid")
        score_k_ready, prob_done = sem("score_k_ready"), sem("prob_done")
        half_done, sum_done = sem("half_done"), sem("sum_done")
        last_half_done, last_sum_done = sem("last_half_done"), sem("last_sum_done")
        pv_done, denom_ready = sem("pv_done"), sem("denom_ready")
        sums_out, sums_turned = sem("sums_out"), sem("sums_turned")
        recip_done, recip_saved = sem("recip_done"), sem("recip_saved")
        recip_spread = [sem(f"recip_spread{g}") for g in range(2)]
        raw_done, heads_done = sem("raw_done"), sem("heads_done")
        proj_ready, proj_done = sem("proj_ready"), sem("proj_done")
        res_biased, res_added = sem("res_biased"), sem("res_added")
        o_stats_done, o_moments_done, o_var_done, o_rstd_done = (
            sem("o_stats_done"), sem("o_moments_done"), sem("o_var_done"), sem("o_rstd_done"))
        scaled_done, result_done = sem("scaled_done"), sem("result_done")

        block = ctx.enter_context(nc.Block())

        @block.sync
        def _(sp):
            def stack_pair(t, d, j):
                rows = slice(HEAD * j, HEAD * (j + 1))
                for n, parts in enumerate((slice(0, 3, 2), slice(1, 3, 1), slice(0, 4, 3))):
                    sp.dma_start(stack[t.parity(d)][HEAD * n:HEAD * (n + 1), :, 2 * j:2 * j + 2, :],
                                 qk_parts[rows, parts, :, :]).then_inc(pair_stacked[j], 16)

            def place_max(t, d, g):
                dst = q_stack[t.parity(d)][STACK:STACK + 1, 4 * g:4 * g + 4, :]
                sp.dma_start(dst.rearrange("o h (t n) -> o (h t) n", n=PARTS),
                             neg_max[:, :]).then_inc(max_placed[g], 16)

            def turn_sums(t):
                need(sp, sums_out, t.count(1, 0))
                for g in range(2):
                    rows = recip[0][g:PARTS:HEAD, :].rearrange("j (c n) -> j c n", c=PARTS // HEADS)
                    sp.dma_start(sums[64 * g:64 * (g + 1), :], rows).then_inc(sums_turned, 16)
                need(sp, recip_done, t.count(1, 0))
                sp.dma_start(recip_rows.rearrange("h (c n) -> (h c) n", c=PARTS // HEADS), sums[:, :]
                             ).then_inc(recip_saved, 16)
                need(sp, recip_saved, t.count(16, 0))
                for g in range(2):
                    rows = recip_rows[4 * g:4 * g + 4, :].unsqueeze(1).to_broadcast([4, HEAD, TOKENS])
                    sp.dma_start(recip[g][:, :], rows).then_inc(recip_spread[g], 16)

            def load_residual(t):
                need(sp, stored, t.count(16, -1))
                b = t.unit(-1) - BATCH * t.layer(-1)
                src = x1 if t.layer(-1) else x
                sp.dma_start(x_res[:], tokens(src, b)).then_inc(res_loaded, 16)

            def store_result(t, d):
                need(sp, result_done, t.count(1, d + 1))
                b = t.unit(d) - BATCH * t.layer(d)
                dst = out if t.layer(d) else x1
                sp.dma_start(tokens(dst, b), x_res[:]).then_inc(stored, 16)

            def step(t):
                if t.has(3):
                    need(sp, h_done, t.count(1, 3))
                    src = x1 if t.layer(3) else x
                    b = t.unit(3) - BATCH * t.layer(3)
                    sp.dma_start(x_in[:], tokens(src, b)).then_inc(x_loaded, 16)
                if t.has(1):
                    need(sp, score_k_ready, t.count(32, 0))
                    stack_pair(t, 1, PAIRS - 1)
                if t.has(0):
                    need(sp, neg_max_done, t.count(2, 1))
                    place_max(t, 0, 1)
                if t.has(-1) and t.layer(-1) and t.layer(-2):
                    load_residual(t)
                if t.has(-1):
                    turn_sums(t)
                if t.has(1):
                    need(sp, neg_max_done, t.count(2, 1, 1))
                    place_max(t, 1, 0)
                change = t.has(-1) and t.layer(-1) and t.layer(-2) == 0
                if change:
                    store_result(t, -2)
                    load_residual(t)
                if t.has(2):
                    need(sp, qk_lo_done, t.count(4, 3))
                    for j in range(PAIRS - 1):
                        if j == 2 and t.has(0):
                            need(sp, score_k_ready, t.count(32, 0, 24))
                        stack_pair(t, 2, j)
                if t.has(-2) and t.layer(-2) == 0 and not change:
                    store_result(t, -2)
                if t.has(-1) and t.layer(-1) == 0:
                    load_residual(t)
                if t.has(-1) and t.layer(-1):
                    store_result(t, -1)

            step(Step(-3))
            sp.dma_start(w_in[0], w_qkv[0].rearrange("(h p) n -> p h n", p=PARTS)).then_inc(w_loaded[0], 16)
            sp.dma_start(adj_in, adj.rearrange("(t p) n -> p t n", p=PARTS)).then_inc(adj_loaded, 16)
            sp.dma_start(w_in[1], w_qkv[1].rearrange("(h p) n -> p h n", p=PARTS)).then_inc(w_loaded[1], 16)
            for n, b_out in enumerate((b_out0, b_out1)):
                sp.dma_start(w_o[n][:], w_out[n].rearrange("(h p) n -> p h n", p=PARTS)).then_inc(consts_loaded, 16)
                sp.dma_start(bias_o[n][:], b_out.partition_broadcast(PARTS)).then_inc(consts_loaded, 16)
            sp.dma_start(bias_v[:], b_v1.partition_broadcast(PARTS)).then_inc(consts_loaded, 16)
            sp.dma_start(gamma_b[:], gamma.partition_broadcast(PARTS)).then_inc(consts_loaded, 16)
            sp.dma_start(beta_b[:], beta.partition_broadcast(PARTS)).then_inc(consts_loaded, 16)
            for n, b in enumerate((b_q1, b_k1)):
                sp.dma_start(bias_qk[:, 2 * n:2 * n + 2], b).then_inc(consts_loaded, 16)

            step(Step(-2))
            run_steps(sp, step, BATCH - 4)
            sp.wait_ge(stored, 16 * UNITS)

        @block.gpsimd
        def _(pool):
            for n, m in enumerate((ident_f, ident_b, ident_h)):
                pool.memset(m[:], 0.0).then_inc(zeroed, 1)
            pool.memset(pick[:], 0.0).then_inc(zeroed, 1)
            pool.memset(minus_half[:], -0.5).then_inc(pool_consts, 1)
            pool.memset(eps[:], EPS).then_inc(pool_consts, 1)
            pool.wait_ge(zeroed, 4)
            for g in range(2):
                pool.memset(pick[:, g, g:g + 1], 1.0).then_inc(pool_consts, 1)
            for m in (ident_f, ident_b, ident_h):
                pool.affine_select(out=m[:], in_=m[:], compare_op=ALU.not_equal, fill=1.0, base=0,
                                   pattern=[[-1, PARTS]], channel_multiplier=1).then_inc(pool_consts, 1)
            pool.wait_ge(pool_consts, POOL_CONSTS)

            def reciprocal_root(t, var_in, var_out, root, semaphores, value):
                pool.tensor_tensor(var_out[:], var_in, eps[:], ALU.add).then_inc(semaphores[0], 1)
                pool.wait_ge(semaphores[0], value)
                pool.tensor_tensor(root[:], var_out[:], minus_half[:], ALU.pow).then_inc(semaphores[1], 1)

            def sum_head(t, h):
                need(pool, prob_done, t.count(32, 0, 4 * h + 4))
                need(pool, sum_done, t.count(8, 0, h))
                pool.tensor_tensor(half_sum[:], prob[:, h, 0:2, :], prob[:, h, 2:4, :], ALU.add).then_inc(half_done, 1)
                pool.wait_ge(half_done, t.count(8, 0, h + 1))
                need(pool, denom_ready, t.count(2, -1, h // 4 + 1))
                pool.tensor_tensor(prob_sum[:, h, :], half_sum[:, 0, :], half_sum[:, 1, :], ALU.add).then_inc(sum_done, 1)

            def bias_residual(t, d):
                need(pool, res_loaded, t.count(16, d + 1))
                for k in range(2):
                    add = twice(bias_o[1] if t.layer(d) else beta_b)
                    pool.tensor_tensor(x_res[:, 2 * k:2 * k + 2, :], x_res[:, 2 * k:2 * k + 2, :], add,
                                       ALU.add).then_inc(res_biased, 1)

            def step(t):
                for s in range(SLOTS):
                    if s == 2 and t.has(-2) and t.layer(-2) == 0:
                        bias_residual(t, -2)
                        need(pool, proj_done, t.count(2, -1))
                        need(pool, res_biased, t.count(2, -1))
                        pool.tensor_tensor(x_res[:], x_res[:], proj[:], ALU.add).then_inc(res_added, 1)
                    if s == 3 and t.has(-2) and t.layer(-2) == 0:
                        need(pool, o_moments_done, t.count(4, -1))
                        need(pool, result_done, t.count(1, -2))
                        reciprocal_root(t, o_moments[:, :, 1], o_var, o_rstd, (o_var_done, o_rstd_done), t.count(1, -1))
                    if s == 4 and t.has(3):
                        need(pool, moments_done, t.count(4, 4))
                        need(pool, h_done, t.count(1, 3))
                        reciprocal_root(t, moments[:, :, 1], var_eps, rstd, (var_done, rstd_done), t.count(1, 4))
                    if s == (3 if t.layer(-2) else 6) and t.has(-1) and t.layer(-1):
                        bias_residual(t, -1)
                    if t.has(0) and not by_vector(t, s):
                        sum_head(t, s)

            step(Step(-3))
            for n in range(2):
                pool.wait_ge(rstd_done, 1)
                pool.memset(k_stack[n][STACK:STACK + 1, :, :], 1.0).then_inc(row_set, 1)
            pool.wait_ge(row_set, 2)
            step(Step(-2))
            pool.wait_ge(consts_loaded, CONSTS)
            run_steps(pool, step)

        @block.scalar
        def _(act):
            def h_of(t, k):
                if k == 0:
                    need(act, shift_done, t.count(1, 3))
                    need(act, h_lo_done, t.count(2, 2))
                for n in (2 * k, 2 * k + 1):
                    last = nc.scalar.activation(h_full[:, n, :], x_in[:, n, :], ACT.Relu,
                                                bias=shift[:, n:n + 1], scale=rstd[:, n:n + 1])
                if k == 1:
                    last.then_inc(h_done, 1)

            def h_high(t, k):
                act.wait_ge(h_done, t.count(1, 3))
                need(act, turned, t.count(2, 2))
                nc.scalar.activation(h_hi[:, 2 * k:2 * k + 2, :], h_full[:, 2 * k:2 * k + 2, :], ACT.Copy
                                     ).then_inc(h_hi_done, 1)

            def qk_of(t, m):
                need(act, qk_ready, t.count(4, 2, m + 1))
                need(act, qk_lo_done, t.count(4, 2, m - 1))
                bias = bias_qk[:, m:m + 1] if t.layer(2) else 0.0
                nc.scalar.activation(qk_full[:, m % 2, :], work[qk_bank(t, m)][:], ACT.Identity, bias=bias,
                                     scale=1.0 / W_SCALE).then_inc(qk_full_done, 1)
                for j in range(PAIRS):
                    need(act, pair_stacked[j], t.count(STACK_DMAS, 2))
                nc.scalar.activation(high(m), work[qk_bank(t, m)][:], ACT.Identity, bias=bias,
                                     scale=1.0 / W_SCALE).then_inc(qk_hi_done, 1)

            def lay_mask(t, n):
                if laid_by(n) == "scalar":
                    need(act, prob_done, exp_before(t, n))
                    nc.scalar.activation(score_k[n % K_BANKS][:], mask_k[:, n % TILES, :], ACT.Copy
                                         ).then_inc(mask_laid, 1)

            def step(t):
                for s in range(SLOTS):
                    for q in range(QUARTERS):
                        if s == 0 and q in (0, 1) and t.has(2):
                            h_of(t, q)
                        if s == 0 and q in (2, 3) and t.has(2):
                            h_high(t, q - 2)
                        if s == 2 and q == 1 and t.has(2):
                            need(act, turned, t.count(2, 3))
                            need(act, v_ready, t.count(2, 1) if t.has(0) else 0)
                            nc.scalar.activation(ht_lo[t.parity(2)][:].rearrange("p h n -> p (h n)"),
                                                 work[0][:].bitcast(F16), ACT.Copy).then_inc(ht_lo_done, 1)
                        if 3 <= s < 3 + QK_TILES and q == 0 and t.has(2):
                            qk_of(t, s - 3)
                        if t.has(0):
                            need(act, score_k_ready, t.count(32, 0, 4 * s + q + 1))
                            if q == 0:
                                need(act, pv_done, t.count(8, -1, 4 * (s // 4 + 1)))
                                need(act, half_done, t.count(8, -1, s + 1))
                            nc.scalar.activation(prob[:, s, q, :], score_k[(4 * s + q) % K_BANKS][:], ACT.Exp,
                                                 scale=1.0 / ROOT).then_inc(prob_done, 1)
                        if (s, q) == (3, 2) and t.has(-1):
                            need(act, denom_ready, t.count(2, 0))
                            need(act, heads_done, t.count(2, -1))
                            nc.scalar.activation(recip[0][:], work[1][:], ACT.Copy).then_inc(sums_out, 1)
                        n = 4 * s + q + K_BANKS
                        if n < 32 and t.has(0):
                            lay_mask(t, n)
                        if (s, q) == (7, 2) and t.has(1):
                            lay_mask(t.next(), 0)
                        if (s, q) == (7, 3) and t.has(1):
                            lay_mask(t.next(), 1)
                            lay_mask(t.next(), 2)
                        if ((s, q) == (3, 3) and t.has(-1)) or ((s, q) == (7, 3) and t.has(0)):
                            need(act, pv_done, t.count(8, 0) if s == 3 else t.count(8, 0, 4))
                            if s == 7:
                                need(act, proj_ready, t.count(2, 0))
                            nc.scalar.activation(heads_t[:, 1 if s == 3 else 0, :], pv[:], ACT.Copy).then_inc(raw_done, 1)

            step(Step(-2))
            act.wait_ge(w_split, 2)
            act.wait_ge(mask_k_done, 2)
            act.wait_ge(consts_loaded, CONSTS)
            act.wait_ge(banks_marked, 1)
            run_steps(act, step)

        @block.vector
        def _(dve):
            tiles_asked = dve.alloc_register("tiles_asked")
            dve.reg_mov(tiles_asked, 0)

            def split_weights(n):
                dve.wait_ge(w_loaded[n], 16)
                nc.vector.tensor_scalar(w_hi[n][:], w_in[n], W_SCALE, None, ALU.mult).then_inc(w_high, 1)
                dve.wait_ge(w_high, n + 1)
                nc.vector.scalar_tensor_tensor(
                    w_lo[n][:].rearrange("p h n -> p (h n)"), w_in[n].rearrange("p h n -> p (h n)"), W_SCALE,
                    w_hi[n][:].rearrange("p h n -> p (h n)"), ALU.mult, ALU.subtract).then_inc(w_split, 1)

            def tile_stats(t, source, st, semaphore, k):
                for n in (2 * k, 2 * k + 1):
                    nc.vector.bn_stats(st[:, n, :], source[:, n, :]).then_inc(semaphore, 1)

            def tile_moments(t, st, mom, semaphores, value):
                dve.wait_ge(semaphores[0], value)
                nc.vector.memset(flag[:], 0.0)
                for n in range(TILES):
                    nc.vector.bn_aggr(mom[:, n, :], st[:, n, :]).then_inc(semaphores[1], 1)

            def max_of(t, s, q):
                if q == 0 and s % 4 == 0:
                    need(dve, max_turned, t.count(2, 0, s // 4 + 1))
                dve.reg_add(tiles_asked, tiles_asked, 1)
                dve.wait_ge(mask_made, 1)
                dve.wait_ge(score_q_ready, tiles_asked)
                nc.vector.tensor_tensor_reduce(out=unused[:, q % 2, :], in0=score_q[q % 2][:], in1=mask_q[:, q, :],
                                               scale=1.0, scalar=-3.0e38, op0=ALU.add, op1=ALU.max,
                                               accum_out=row_max[:, s, q:q + 1]).then_inc(max_done, 1)

            def negate_max(t, d, g):
                need(dve, max_turned, t.count(2, d, g + 1))
                need(dve, max_placed[1 - g], t.count(16, d, 16 * g))
                nc.vector.tensor_scalar(neg_max[:], work[1 - g][0:4 * TILES, 0:PARTS], -1.0, None,
                                        ALU.mult).then_inc(neg_max_done, 1)

            def reciprocals(t):
                need(dve, sums_turned, t.count(32, 0))
                nc.vector.reciprocal(sums[:], sums[:]).then_inc(recip_done, 1)

            def normalise(t, d, g):
                need(dve, recip_spread[g], t.count(16, d + 1))
                need(dve, raw_done, t.count(2, d, g + 1))
                nc.vector.tensor_tensor(heads_t[:, g, :], heads_t[:, g, :], recip[g][:], ALU.mult).then_inc(heads_done, 1)

            def take_v(t, k):
                need(dve, v_ready, t.count(2, 0, k + 1))
                need(dve, pv_done, t.count(8, -1))
                dst = v[t.parity(0)][:, 2 * k:2 * k + 2, :]
                bank = work[1 - k][:].rearrange("p (t n) -> p t n", t=2)
                if t.layer(0):
                    nc.vector.scalar_tensor_tensor(dst, bank, 1.0 / W_SCALE, twice(bias_v),
                                                   ALU.mult, ALU.add).then_inc(v_done, 1)
                else:
                    nc.vector.tensor_scalar(dst, bank, 1.0 / W_SCALE, None, ALU.mult).then_inc(v_done, 1)

            def take_projection(t, k):
                need(dve, proj_ready, t.count(2, -1, k + 1))
                tiles = slice(2 * k, 2 * k + 2)
                bank = work[1 - k][:].rearrange("p (t n) -> p t n", t=2)
                if t.layer(-1):
                    need(dve, res_biased, t.count(2, -1, k + 1))
                    nc.vector.tensor_tensor(x_res[:, tiles, :], bank, x_res[:, tiles, :], ALU.add
                                            ).then_inc(proj_done, 1)
                    if k == 1:
                        need(dve, proj_done, t.count(2, 0))
                        nc.vector.memset(flag[:], 0.0).then_inc(result_done, 1)
                else:
                    need(dve, result_done, t.count(1, -1))
                    nc.vector.tensor_tensor(proj[:, tiles, :], bank, twice(bias_o[0]), ALU.add).then_inc(proj_done, 1)

            def scale_0(t, k):
                need(dve, res_added, t.count(1, -1))
                for n in (2 * k, 2 * k + 1):
                    nc.vector.scalar_tensor_tensor(proj[:, n, :], proj[:, n, :], o_moments[:, n, 0:1], gamma_b[:],
                                                   ALU.subtract, ALU.mult).then_inc(scaled_done, 1)

            def finish_0(t, k):
                need(dve, o_rstd_done, t.count(1, -1))
                for n in (2 * k, 2 * k + 1):
                    need(dve, scaled_done, t.count(4, -2, n + 1))
                    last = nc.vector.scalar_tensor_tensor(x_res[:, n, :], proj[:, n, :], o_rstd[:, n:n + 1],
                                                          x_res[:, n, :], ALU.mult, ALU.add)
                if k == 1:
                    last.then_inc(result_done, 1)

            def work_of(t, s, q):
                at = (s, q)
                finishing = t.has(-2) and t.layer(-2) == 0
                if at == (0, 0) and finishing:
                    need(dve, proj_done, t.count(2, -1))
                    need(dve, o_moments_done, t.count(4, -2))
                    tile_stats(t, proj, o_stats, o_stats_done, 0)
                if at == (0, 2) and finishing:
                    tile_stats(t, proj, o_stats, o_stats_done, 1)
                if at == (0, 1) and t.has(0):
                    negate_max(t, 0, 1)
                if at in ((0, 3), (1, 1)) and t.has(2):
                    k = s
                    need(dve, h_hi_done, t.count(2, 2, k + 1))
                    need(dve, turned, t.count(2, 2))
                    tiles = slice(2 * k, 2 * k + 2)
                    nc.vector.tensor_tensor(h_lo[:, tiles, :], h_full[:, tiles, :], h_hi[:, tiles, :], ALU.subtract
                                            ).then_inc(h_lo_done, 1)
                if at == (1, 0) and t.has(0):
                    take_v(t, 0)
                if at == (1, 2) and t.has(0):
                    take_v(t, 1)
                if at == (3, 1) and finishing:
                    need(dve, scaled_done, t.count(4, -2))
                    need(dve, o_rstd_done, t.count(1, -2))
                    tile_moments(t, o_stats, o_moments, (o_stats_done, o_moments_done), t.count(4, -1))
                if at in ((2, 0), (2, 1)) and t.has(2):
                    need(dve, turned, t.count(2, 2, 1))
                    need(dve, v_ready, t.count(2, 1) if t.has(0) else 0)
                    nc.vector.tensor_copy(ht_hi[t.parity(2)][:, q, :],
                                          work[1][:].bitcast(F16).rearrange("p (h n) -> p h n", h=HALVES)[:, q, :]
                                          ).then_inc(ht_hi_done, 1)
                if 3 <= s < 3 + QK_TILES and q == (1 if s > 5 else 2) and t.has(2):
                    m = s - 3
                    need(dve, qk_hi_done, t.count(4, 2, m + 1))
                    for j in range(PAIRS):
                        need(dve, pair_stacked[j], t.count(STACK_DMAS, 2))
                    nc.vector.tensor_tensor(low(m), qk_full[:, m % 2, :], high(m),
                                            ALU.subtract).then_inc(qk_lo_done, 1)
                if at == (5, 3) and t.has(-1):
                    normalise(t, -1, 0)
                if at == (4, 0) and t.has(3):
                    need(dve, x_loaded, t.count(16, 4))
                    need(dve, moments_done, t.count(4, 3))
                    tile_stats(t, x_in, stats, stats_done, 0)
                if at == (4, 1) and t.has(3):
                    tile_stats(t, x_in, stats, stats_done, 1)
                if at == (5, 1) and t.has(1):
                    negate_max(t, 1, 0)
                if at == (4, 2) and t.has(-1):
                    reciprocals(t)
                if at == (4, 3) and t.has(3):
                    need(dve, shift_done, t.count(1, 3))
                    tile_moments(t, stats, moments, (stats_done, moments_done), t.count(4, 4))
                if at == (6, 0) and t.has(-1):
                    normalise(t, -1, 1)
                last = t.i is None and t.c == BATCH + 1
                places = ((4, 3), (5, 0), (5, 1), (5, 2)) if last else ((6, 1), (6, 3), (7, 0), (7, 1))
                for k, place in enumerate(places):
                    if at == place and finishing:
                        scale_0(t, k) if k < 2 else finish_0(t, k - 2)
                if at == (7, 2) and t.has(-1):
                    take_projection(t, 0)
                if at == (7, 3) and t.has(3):
                    need(dve, rstd_done, t.count(1, 4))
                    nc.vector.scalar_tensor_tensor(shift[:], moments[:, :, 0], -1.0, rstd[:],
                                                   ALU.mult, ALU.mult).then_inc(shift_done, 1)

            def sum_last(t, h):
                half = x_in[:].rearrange("p t d -> p (t d)").rearrange("p (t n) -> p t n", t=2)
                need(dve, prob_done, t.count(32, 0, 4 * h + 4))
                need(dve, last_sum_done, h - 4)
                nc.vector.tensor_tensor(half, prob[:, h, 0:2, :], prob[:, h, 2:4, :], ALU.add).then_inc(last_half_done, 1)
                need(dve, last_half_done, h - 3)
                need(dve, denom_ready, t.count(2, 0))
                nc.vector.tensor_tensor(prob_sum[:, h, :], half[:, 0, :], half[:, 1, :], ALU.add
                                        ).then_inc(last_sum_done, 1)

            def step(t):
                for s in range(SLOTS):
                    for q in range(QUARTERS):
                        if q == 3 and by_vector(t, s):
                            sum_last(t, s)
                        if t.has(1):
                            max_of(t, s, q)
                        work_of(t, s, q)
                if t.has(-1):
                    take_projection(t, 1)

            step(Step(-3))
            split_weights(0)
            dve.wait_ge(adj_loaded, 16)
            nc.vector.tensor_scalar(mask_q[:], adj_in, 0.0, MASKED, ALU.is_equal, ALU.mult).then_inc(mask_made, 1)
            step(Step(-2))
            for n in range(2):
                dve.wait_ge(mask_turned, n + 1)
                nc.vector.tensor_copy(mask_k[:, 2 * n:2 * n + 2, :].rearrange("p t n -> p (t n)"),
                                      score_q[n][:].bitcast(BF16)).then_inc(mask_k_done, 1)
            split_weights(1)
            dve.wait_ge(mask_k_done, 2)
            dve.wait_ge(consts_loaded, CONSTS)
            dve.wait_ge(pool_consts, POOL_CONSTS)
            dve.wait_ge(banks_marked, 1)
            run_steps(dve, step)

        @block.tensor
        def _(pe):
            def scores_by_key(t, s, q):
                if s % 4 == 0 and q == 0:
                    need(pe, max_placed[s // 4], t.count(16, 1))
                bank = score_k[(4 * s + q) % K_BANKS]
                laid = laid_by(4 * s + q) == "scalar"
                if laid:
                    by_scalar = [n for n in range(TILES * SLOTS) if laid_by(n) == "scalar"]
                    need(pe, mask_laid, t.count(len(by_scalar), 0, by_scalar.index(4 * s + q) + 1))
                else:
                    need(pe, prob_done, exp_before(t, 4 * s + q))
                    nc.tensor.matmul(bank[:], ident_b[:], mask_k[:, q, :], start=True, stop=False)
                nc.tensor.matmul(bank[:], k_stack[t.parity(0)][0:STACK + 1, s, PARTS * q:PARTS * (q + 1)],
                                 q_stack[t.parity(0)][0:STACK + 1, s, :], start=False, stop=True,
                                 skip_group_check=laid).then_inc(score_k_ready, 1)

            def scores_by_query(t, s, q):
                if s % 2 == 0 and q == 0:
                    need(pe, pair_stacked[s // 2], t.count(STACK_DMAS, 2))
                need(pe, max_done, t.count(32, 1, 4 * s + q - 1))
                nc.tensor.matmul(score_q[q % 2][:], q_stack[t.parity(1)][0:STACK, s, PARTS * q:PARTS * (q + 1)],
                                 k_stack[t.parity(1)][0:STACK, s, :], start=True, stop=True
                                 ).then_inc(score_q_ready, 1)

            def times_v(t, d, g, k):
                if k == 0:
                    need(pe, prob_done, t.count(32, d, 16 * (g + 1)))
                    need(pe, v_done, t.count(2, d + 1))
                    need(pe, raw_done, t.count(2, d, g))
                for j in range(4):
                    h = 4 * g + j
                    last = nc.tensor.matmul(pv[HEAD * j:HEAD * (j + 1), :], v[t.parity(d)][:, k, HEAD * h:HEAD * (h + 1)],
                                            prob[:, h, k, :], start=(k == 0), stop=(k == TILES - 1))
                last.then_inc(pv_done, 1)

            def sum_rows(t, d, g):
                if t.i is None and t.c + d == UNITS - 1 and g == 1:
                    need(pe, last_sum_done, 4)
                else:
                    need(pe, sum_done, t.count(8, d, 4 * (g + 1)))
                for j in range(4):
                    last = nc.tensor.matmul(work[1][HEAD * j:HEAD * (j + 1), :], pick[:, g, :],
                                            prob_sum[:, 4 * g + j, :], start=(g == 0), stop=(g == 1))
                last.then_inc(denom_ready, 1)

            def turn_h(t, part, bank):
                dst = work[bank][:].bitcast(F16).rearrange("p (h n) -> p h n", h=HALVES)
                for k in range(HALVES):
                    for n in range(TILES):
                        last = nc.tensor.transpose(dst[:, k, PARTS * n:PARTS * (n + 1)],
                                                   part[:, n, PARTS * k:PARTS * (k + 1)], ident_h[:])
                last.then_inc(turned, 1)

            def qk_terms(t):
                hi, lo = w_hi[t.layer(2)], w_lo[t.layer(2)]
                p = t.parity(2)
                return [(w, ht, k) for w, ht in ((hi, ht_hi[p]), (lo, ht_hi[p]), (hi, ht_lo[p])) for k in range(HALVES)]

            def project_qk(t, m, part):
                terms = qk_terms(t)
                for n in range(3 * part, 3 * part + 3):
                    w, ht, k = terms[n]
                    last = nc.tensor.matmul(work[qk_bank(t, m)][:], w[:, k, PARTS * m:PARTS * (m + 1)], ht[:, k, :],
                                            start=(n == 0), stop=(n == 5))
                if part == 1:
                    last.then_inc(qk_ready, 1)

            def project_v(t, n):
                hi, lo = w_hi[t.layer(0)], w_lo[t.layer(0)]
                p = t.parity(0)
                terms = [(w, ht, k) for w, ht in ((hi, ht_hi[p]), (lo, ht_hi[p]), (hi, ht_lo[p])) for k in range(HALVES)]
                dst = work[1 - n // 2][:].rearrange("p (t n) -> p t n", t=2)[:, n % 2, :]
                for i, (w, ht, k) in enumerate(terms):
                    last = nc.tensor.matmul(dst, ht[:, k, PARTS * n:PARTS * (n + 1)], w[:, k, 2 * DIM:3 * DIM],
                                            start=(i == 0), stop=(i == 5))
                if n % 2:
                    last.then_inc(v_ready, 1)

            def turn_max(t, d, g):
                need(pe, max_done, t.count(32, d, 16 * (g + 1)))
                nc.tensor.matmul(work[1 - g][0:4 * TILES, 0:PARTS],
                                 row_max[:, 4 * g:4 * g + 4, :].rearrange("p h t -> p (h t)"), ident_f[:],
                                 start=True, stop=True).then_inc(max_turned, 1)

            def project_out(t, n):
                dst = work[1 - n // 2][:].rearrange("p (t n) -> p t n", t=2)[:, n % 2, :]
                for half in range(HALVES):
                    last = nc.tensor.matmul(dst, heads_t[:, half, PARTS * n:PARTS * (n + 1)],
                                            w_o[t.layer(-1)][:, half, :], start=(half == 0), stop=(half == 1))
                if n % 2:
                    last.then_inc(proj_ready, 1)

            def banks_free(t):
                for semaphore, per, d, extra in ((ht_hi_done, 2, 2, 0), (ht_lo_done, 1, 2, 0), (qk_hi_done, 4, 2, 0),
                                                 (v_done, 2, 0, 0), (neg_max_done, 2, 0, 1), (proj_done, 2, -1, 0)):
                    need(pe, semaphore, min(t.count(per, d, extra), per * UNITS))

            def step(t):
                if t.i is None and (t.c < 2 or t.c > UNITS - 4):
                    banks_free(t)
                for s in range(SLOTS):
                    for q in range(QUARTERS):
                        if t.has(0):
                            scores_by_key(t, s, q)
                        if t.has(1):
                            scores_by_query(t, s, q)
                        if (s, q) == (0, 1) and t.has(0):
                            need(pe, proj_done, t.count(2, -1))
                            turn_max(t, 0, 1)
                        if (s, q) in ((0, 1), (1, 1), (2, 1), (3, 0)) and t.has(-1):
                            times_v(t, -1, 1, s)
                        if q == 1 and s >= 4 and t.has(0):
                            times_v(t, 0, 0, s - 4)
                        if (s, q) == (0, 0) and t.has(0):
                            need(pe, proj_done, t.count(2, -1, -1))
                            project_v(t, 0)
                        if (s, q) == (0, 2) and t.has(0):
                            project_v(t, 1)
                        if (s, q) == (0, 3) and t.has(0):
                            need(pe, neg_max_done, t.count(2, 1))
                            project_v(t, 2)
                        if (s, q) == (1, 0) and t.has(0):
                            project_v(t, 3)
                        if (s, q) == (1, 2) and t.has(2):
                            need(pe, h_hi_done, t.count(2, 3))
                            need(pe, v_done, t.count(2, 0, 1))
                            turn_h(t, h_hi, 1)
                        if (s, q) == (2, 0) and t.has(2):
                            need(pe, h_lo_done, t.count(2, 3))
                            need(pe, v_done, t.count(2, 1) if t.has(0) else 0)
                            turn_h(t, h_lo, 0)
                        for n, place in enumerate(QK_AT):
                            if (s, q) == place and t.has(2):
                                m, part = divmod(n, 2)
                                if n == 0:
                                    need(pe, ht_hi_done, t.count(2, 3))
                                    need(pe, ht_lo_done, t.count(1, 3))
                                elif part == 0:
                                    need(pe, qk_hi_done, t.count(4, 2, m - qk_bank(t, 1)))
                                project_qk(t, m, part)
                        if (s, q) in ((2, 3), (3, 1)) and t.has(-1):
                            if s == 2:
                                if t.has(2):
                                    need(pe, ht_hi_done, t.count(2, 3))
                                elif t.has(0):
                                    need(pe, v_done, t.count(2, 1))
                            sum_rows(t, -1, s - 2)
                        if (s, q) == (5, 1) and t.has(1):
                            if t.has(-1):
                                need(pe, sums_out, t.count(1, 0))
                            elif t.has(2):
                                need(pe, ht_hi_done, t.count(2, 3))
                            turn_max(t, 1, 0)
                        if (s, q) in ((6, 2), (6, 3), (7, 0), (7, 2)) and t.has(-1):
                            n = ((6, 2), (6, 3), (7, 0), (7, 2)).index((s, q))
                            if n == 0:
                                need(pe, heads_done, t.count(2, 0))
                                if t.has(1):
                                    need(pe, neg_max_done, t.count(2, 1, 1))
                                else:
                                    need(pe, sums_out, t.count(1, 0))
                            if n == 2:
                                if t.has(2):
                                    need(pe, qk_hi_done, t.count(4, 3))
                                elif t.has(0):
                                    need(pe, v_done, t.count(2, 1))
                            project_out(t, n)

            pe.wait_ge(pool_consts, POOL_CONSTS)
            pe.wait_ge(w_split, 1)
            step(Step(-2))
            pe.wait_ge(mask_made, 1)
            for n in range(2):
                turned_mask = score_q[n][:].bitcast(BF16).rearrange("p (t n) -> p t n", t=2)
                for k in range(2):
                    for q in range(TILES):
                        key = PARTS * (2 * n + k)
                        last = nc.tensor.transpose(turned_mask[:, k, PARTS * q:PARTS * (q + 1)],
                                                   mask_q[:, q, key:key + PARTS], ident_b[:])
                last.then_inc(mask_turned, 1)
            pe.wait_ge(mask_k_done, 2)
            for bank in score_k:
                last = nc.tensor.matmul(bank[:], ident_b[:], mask_k[:, 0, :], start=True, stop=True)
            last.then_inc(banks_marked, 1)
            pe.wait_ge(w_split, 2)
            pe.wait_ge(row_set, 2)
            pe.wait_ge(consts_loaded, CONSTS)
            run_steps(pe, step)


def kernel(**inputs):
    import numpy as np
    import concourse.bacc as bacc
    from concourse import mybir
    from concourse.bass_utils import run_bass_kernel_spmd

    def even_odd(w):
        return np.concatenate([w.reshape(DIM, PAIRS, 2, HEAD)[:, :, g, :].reshape(DIM, -1) for g in range(2)], 1)

    def by_head_tile(b):
        return np.ascontiguousarray(b.reshape(PAIRS, 2, HEAD).transpose(0, 2, 1).reshape(-1, 2))

    a = {name: np.asarray(value) for name, value in inputs.items()}
    w0 = a["L0_gnn_w_qkv"]
    arrays = {
        "x": a["x"], "adj": a["adj"],
        "w_qkv0": np.concatenate([even_odd(w0[:, :DIM]), even_odd(w0[:, DIM:2 * DIM]), w0[:, 2 * DIM:]], 1),
        "w_out0": a["L0_gnn_w_proj"], "b_out0": a["L0_gnn_b_proj"],
        "gamma": a["L0_gnn_ln_gamma"], "beta": a["L0_gnn_ln_beta"],
        "w_qkv1": np.concatenate([even_odd(a["L1_gnn_Wq"]), even_odd(a["L1_gnn_Wk"]), a["L1_gnn_Wv"]], 1),
        "b_q1": by_head_tile(a["L1_gnn_bq"]), "b_k1": by_head_tile(a["L1_gnn_bk"]), "b_v1": a["L1_gnn_bv"],
        "w_out1": a["L1_gnn_Wo"], "b_out1": a["L1_gnn_bo"],
    }
    nc = bacc.Bacc("TRN2", target_bir_lowering=False, num_devices=1)
    args = {}
    for name, value in arrays.items():
        arrays[name] = np.ascontiguousarray(value)
        args[name] = nc.dram_tensor(name, value.shape, mybir.dt.from_np(value.dtype), kind="ExternalInput").ap()
    out = nc.dram_tensor("out", (BATCH, TOKENS, DIM), mybir.dt.float32, kind="ExternalOutput").ap()
    build(nc, out=out, **args)
    r = run_bass_kernel_spmd(nc, [arrays], core_ids=[0])
    return r.results[0]["out"]
```
